# Optimizing a Trainium2 kernel written in Bass

```python
import numpy as np
import jax
import jax.numpy as jnp

def _softmax(x, axis=-1):
    return jax.nn.softmax(x, axis=axis)

def _gelu(x):
    return jax.nn.gelu(x, approximate=True)

def _silu(x):
    return jax.nn.silu(x)

def _sigmoid(x):
    return jax.nn.sigmoid(x)

def _layernorm(x, axis=-1, eps=1e-05):
    m = jnp.mean(x, axis=axis, keepdims=True)
    v = jnp.var(x, axis=axis, keepdims=True)
    return (x - m) / jnp.sqrt(v + eps)

def _scatter_add(tgt, idx, src, axis=0):
    return tgt.at[idx].add(src)

def _segment_sum(src, seg, n):
    return jax.ops.segment_sum(src, seg, n)
kernel_name = 'mk_adaln_d1_jaxref_r8_30a799'

def setup_inputs(seed: int=0):
    np.random.seed(seed)
    _w = jnp.asarray

    def _L0_attn_setup():
        import jax, jax.numpy as jnp
        import numpy as np
        D_MODEL = 128
        D_STATE = 16
        B, L = (4, 512)
        LN_EPS = 1e-05
        key = jax.random.key(seed)
        ks = jax.random.split(key, 7)
        s = 1.0 / np.sqrt(D_MODEL)
        return {'x': jax.random.normal(ks[0], (B, L, D_MODEL), jnp.float32), 'W_in': jax.random.normal(ks[1], (2 * D_MODEL, D_MODEL), jnp.float32) * s, 'W_x': jax.random.normal(ks[2], (2 * D_STATE + 1, D_MODEL), jnp.float32) * s, 'W_dt': jax.random.normal(ks[3], (D_MODEL, 1), jnp.float32), 'b_dt': jax.random.normal(ks[4], (D_MODEL,), jnp.float32) * 0.1, 'gamma': jnp.ones((D_MODEL,), jnp.float32), 'beta': jnp.zeros((D_MODEL,), jnp.float32)}
    _L0_attn_in = _L0_attn_setup()

    def _L0_ffn_setup():
        import jax, jax.numpy as jnp
        import numpy as np
        DIM = 128
        DEPTH = 2
        HEADS = 8
        DIM_HEAD = 64
        WINDOW = 64
        INNER = HEADS * DIM_HEAD
        HID = int(DIM * 4 * 2 / 3)
        B, N = (2, 1024)
        QK_SCALE = 8.0

        def shift_token(t):
            t1, t2 = jnp.split(t, 2, axis=-1)
            t2 = jnp.pad(t2, ((0, 0), (1, 0), (0, 0)))[:, :-1]
            return jnp.concatenate([t1, t2], axis=-1)

        def l2norm(t):
            return t / jnp.clip(jnp.linalg.norm(t, axis=-1, keepdims=True), 1e-12)

        def rotate_half(x):
            x1, x2 = jnp.split(x, 2, axis=-1)
            return jnp.concatenate([-x2, x1], axis=-1)

        def rotary_xpos(q, k):
            n = q.shape[-2]
            half_idx = jnp.arange(0, DIM_HEAD, 2, dtype=jnp.float32)
            inv_freq = 1.0 / 10000.0 ** (half_idx / DIM_HEAD)
            t = jnp.arange(n, dtype=jnp.float32)
            freqs = t[:, None] * inv_freq[None, :]
            freqs = jnp.concatenate([freqs, freqs], axis=-1)
            base = (half_idx + 0.4 * DIM_HEAD) / (1.4 * DIM_HEAD)
            power = (t - n // 2) / float(WINDOW // 2)
            scale = base[None, :] ** power[:, None]
            scale = jnp.concatenate([scale, scale], axis=-1)
            cos, sin = (jnp.cos(freqs), jnp.sin(freqs))
            q = q * cos * scale + rotate_half(q) * sin * scale
            k = k * cos / scale + rotate_half(k) * sin / scale
            return (q, k)

        def local_attention(q, k, v):
            b, h, n, d = q.shape
            w = n // WINDOW
            bq = q.reshape(b, h, w, WINDOW, d) * QK_SCALE
            bk = k.reshape(b, h, w, WINDOW, d)
            bv = v.reshape(b, h, w, WINDOW, d)

            def look_around(t):
                p = jnp.pad(t, ((0, 0), (0, 0), (1, 0), (0, 0), (0, 0)))
                return jnp.concatenate([p[:, :, :w], p[:, :, 1:]], axis=3)
            bk, bv = (look_around(bk), look_around(bv))
            bt = jnp.arange(n).reshape(w, WINDOW)
            btp = jnp.pad(bt, ((1, 0), (0, 0)), constant_values=-1)
            btk = jnp.concatenate([btp[:w], btp[1:]], axis=1)
            sim = jnp.einsum('bhwid,bhwjd->bhwij', bq, bk)
            i = bt[:, :, None]
            j = btk[:, None, :]
            mask = (i < j) | (i > j + WINDOW) | (j == -1)
            sim = jnp.where(mask, -jnp.finfo(sim.dtype).max, sim)
            attn = jax.nn.softmax(sim, axis=-1)
            out = jnp.einsum('bhwij,bhwjd->bhwid', attn, bv)
            return out.reshape(b, h, n, d)

        def _layer(x, wqkv, qs, ksc, wo, lg, lb, w1, b1, w2, b2):
            b, n, _ = x.shape
            h = shift_token(x)
            qkv = h @ wqkv
            q, k, v = jnp.split(qkv, 3, axis=-1)
            to_heads = lambda t: t.reshape(b, n, HEADS, DIM_HEAD).transpose(0, 2, 1, 3)
            q, k, v = (to_heads(q), to_heads(k), to_heads(v))
            q = l2norm(q) * qs
            k = l2norm(k) * ksc
            q, k = rotary_xpos(q, k)
            o = local_attention(q, k, v)
            o = o.transpose(0, 2, 1, 3).reshape(b, n, INNER)
            x = x + o @ wo
            h = shift_token(x)
            mu = h.mean(-1, keepdims=True)
            var = h.var(-1, keepdims=True)
            h = (h - mu) / jnp.sqrt(var + 1e-05) * lg + lb
            h = h @ w1 + b1
            a, g = jnp.split(h, 2, axis=-1)
            h = a * jax.nn.gelu(g, approximate=False)
            x = x + h @ w2 + b2
            return x
        key = jax.random.key(seed)
        ks = jax.random.split(key, 6)
        return {'x': jax.random.normal(ks[0], (B, N, DIM), jnp.float32), 'wqkv': jax.random.normal(ks[1], (DEPTH, DIM, 3 * INNER), jnp.float32) * 0.02, 'q_scale': jnp.ones((DEPTH, DIM_HEAD), jnp.float32), 'k_scale': jnp.ones((DEPTH, DIM_HEAD), jnp.float32), 'wo': jax.random.normal(ks[2], (DEPTH, INNER, DIM), jnp.float32) * 0.02, 'ln_g': jnp.ones((DEPTH, DIM), jnp.float32), 'ln_b': jnp.zeros((DEPTH, DIM), jnp.float32), 'w1': jax.random.normal(ks[3], (DEPTH, DIM, 2 * HID), jnp.float32) * 0.02, 'b1': jnp.zeros((DEPTH, 2 * HID), jnp.float32), 'w2': jax.random.normal(ks[4], (DEPTH, HID, DIM), jnp.float32) * 0.02, 'b2': jnp.zeros((DEPTH, DIM), jnp.float32)}
    _L0_ffn_in = _L0_ffn_setup()
    _L0_c = _w((lambda *s: np.random.randn(*s).astype(np.float32) * 0.05)(32, 128))
    _L0_wmod = _w((lambda *s: np.random.randn(*s).astype(np.float32) * 0.05)(128, 6 * 128) * 128 ** (-0.5))
    _d = {'L0_attn_x': _L0_attn_in['x'], 'L0_attn_W_in': _L0_attn_in['W_in'], 'L0_attn_W_x': _L0_attn_in['W_x'], 'L0_attn_W_dt': _L0_attn_in['W_dt'], 'L0_attn_b_dt': _L0_attn_in['b_dt'], 'L0_attn_gamma': _L0_attn_in['gamma'], 'L0_attn_beta': _L0_attn_in['beta'], 'L0_ffn_wqkv': _L0_ffn_in['wqkv'], 'L0_ffn_q_scale': _L0_ffn_in['q_scale'], 'L0_ffn_k_scale': _L0_ffn_in['k_scale'], 'L0_ffn_wo': _L0_ffn_in['wo'], 'L0_ffn_ln_g': _L0_ffn_in['ln_g'], 'L0_ffn_ln_b': _L0_ffn_in['ln_b'], 'L0_ffn_w1': _L0_ffn_in['w1'], 'L0_ffn_b1': _L0_ffn_in['b1'], 'L0_ffn_w2': _L0_ffn_in['w2'], 'L0_ffn_b2': _L0_ffn_in['b2'], 'L0_c': _L0_c, 'L0_wmod': _L0_wmod}
    _x0 = _d['L0_attn_x']
    _d['L0_attn_x'] = jax.random.normal(jax.random.fold_in(jax.random.key(seed), 1), (32, 256, 128), dtype=_x0.dtype)
    del _x0
    return _d

def reference(L0_attn_x, L0_attn_W_in, L0_attn_W_x, L0_attn_W_dt, L0_attn_b_dt, L0_attn_gamma, L0_attn_beta, L0_ffn_wqkv, L0_ffn_q_scale, L0_ffn_k_scale, L0_ffn_wo, L0_ffn_ln_g, L0_ffn_ln_b, L0_ffn_w1, L0_ffn_b1, L0_ffn_w2, L0_ffn_b2, L0_c, L0_wmod):

    def _L0_attn_ref(x, W_in, W_x, W_dt, b_dt, gamma, beta):
        import jax, jax.numpy as jnp
        import numpy as np
        D_MODEL = 128
        D_STATE = 16
        B, L = (4, 512)
        LN_EPS = 1e-05
        xz = jnp.einsum('bld,ed->ble', x, W_in)
        x_in, z = jnp.split(xz, 2, axis=-1)
        x_in = jnp.tanh(x_in)
        z = jax.nn.sigmoid(z)
        dt_raw = jnp.einsum('bld,sd->bls', x_in, W_x)[..., :1]
        dt = jax.nn.sigmoid(dt_raw * W_dt[:, 0] + b_dt)
        a = jnp.exp(-jax.nn.softplus(dt))

        def step(h, inp):
            a_t, x_t = inp
            h = a_t * h + (1.0 - a_t) * x_t
            return (h, h)
        h0 = jnp.zeros((x.shape[0], x.shape[2]), x.dtype)
        _, ys = jax.lax.scan(step, h0, (jnp.swapaxes(a, 0, 1), jnp.swapaxes(x_in, 0, 1)))
        y = jnp.swapaxes(ys, 0, 1)
        g = y * z
        mu = jnp.mean(g, axis=-1, keepdims=True)
        var = jnp.var(g, axis=-1, keepdims=True)
        ln = (g - mu) / jnp.sqrt(var + LN_EPS) * gamma + beta
        return ln + x

    def _L0_ffn_ref(x, wqkv, q_scale, k_scale, wo, ln_g, ln_b, w1, b1, w2, b2):
        import jax, jax.numpy as jnp
        import numpy as np
        DIM = 128
        DEPTH = 2
        HEADS = 8
        DIM_HEAD = 64
        WINDOW = 64
        INNER = HEADS * DIM_HEAD
        HID = int(DIM * 4 * 2 / 3)
        B, N = (2, 1024)
        QK_SCALE = 8.0

        def shift_token(t):
            t1, t2 = jnp.split(t, 2, axis=-1)
            t2 = jnp.pad(t2, ((0, 0), (1, 0), (0, 0)))[:, :-1]
            return jnp.concatenate([t1, t2], axis=-1)

        def l2norm(t):
            return t / jnp.clip(jnp.linalg.norm(t, axis=-1, keepdims=True), 1e-12)

        def rotate_half(x):
            x1, x2 = jnp.split(x, 2, axis=-1)
            return jnp.concatenate([-x2, x1], axis=-1)

        def rotary_xpos(q, k):
            n = q.shape[-2]
            half_idx = jnp.arange(0, DIM_HEAD, 2, dtype=jnp.float32)
            inv_freq = 1.0 / 10000.0 ** (half_idx / DIM_HEAD)
            t = jnp.arange(n, dtype=jnp.float32)
            freqs = t[:, None] * inv_freq[None, :]
            freqs = jnp.concatenate([freqs, freqs], axis=-1)
            base = (half_idx + 0.4 * DIM_HEAD) / (1.4 * DIM_HEAD)
            power = (t - n // 2) / float(WINDOW // 2)
            scale = base[None, :] ** power[:, None]
            scale = jnp.concatenate([scale, scale], axis=-1)
            cos, sin = (jnp.cos(freqs), jnp.sin(freqs))
            q = q * cos * scale + rotate_half(q) * sin * scale
            k = k * cos / scale + rotate_half(k) * sin / scale
            return (q, k)

        def local_attention(q, k, v):
            b, h, n, d = q.shape
            w = n // WINDOW
            bq = q.reshape(b, h, w, WINDOW, d) * QK_SCALE
            bk = k.reshape(b, h, w, WINDOW, d)
            bv = v.reshape(b, h, w, WINDOW, d)

            def look_around(t):
                p = jnp.pad(t, ((0, 0), (0, 0), (1, 0), (0, 0), (0, 0)))
                return jnp.concatenate([p[:, :, :w], p[:, :, 1:]], axis=3)
            bk, bv = (look_around(bk), look_around(bv))
            bt = jnp.arange(n).reshape(w, WINDOW)
            btp = jnp.pad(bt, ((1, 0), (0, 0)), constant_values=-1)
            btk = jnp.concatenate([btp[:w], btp[1:]], axis=1)
            sim = jnp.einsum('bhwid,bhwjd->bhwij', bq, bk)
            i = bt[:, :, None]
            j = btk[:, None, :]
            mask = (i < j) | (i > j + WINDOW) | (j == -1)
            sim = jnp.where(mask, -jnp.finfo(sim.dtype).max, sim)
            attn = jax.nn.softmax(sim, axis=-1)
            out = jnp.einsum('bhwij,bhwjd->bhwid', attn, bv)
            return out.reshape(b, h, n, d)

        def _layer(x, wqkv, qs, ksc, wo, lg, lb, w1, b1, w2, b2):
            b, n, _ = x.shape
            h = shift_token(x)
            qkv = h @ wqkv
            q, k, v = jnp.split(qkv, 3, axis=-1)
            to_heads = lambda t: t.reshape(b, n, HEADS, DIM_HEAD).transpose(0, 2, 1, 3)
            q, k, v = (to_heads(q), to_heads(k), to_heads(v))
            q = l2norm(q) * qs
            k = l2norm(k) * ksc
            q, k = rotary_xpos(q, k)
            o = local_attention(q, k, v)
            o = o.transpose(0, 2, 1, 3).reshape(b, n, INNER)
            x = x + o @ wo
            h = shift_token(x)
            mu = h.mean(-1, keepdims=True)
            var = h.var(-1, keepdims=True)
            h = (h - mu) / jnp.sqrt(var + 1e-05) * lg + lb
            h = h @ w1 + b1
            a, g = jnp.split(h, 2, axis=-1)
            h = a * jax.nn.gelu(g, approximate=False)
            x = x + h @ w2 + b2
            return x
        for l in range(DEPTH):
            x = _layer(x, wqkv[l], q_scale[l], k_scale[l], wo[l], ln_g[l], ln_b[l], w1[l], b1[l], w2[l], b2[l])
        return x
    x = L0_attn_x
    mod = (_silu(L0_c) @ L0_wmod).reshape(L0_c.shape[0], 6, 1, -1)
    sa, ca, ga, sb, cb, gb = (mod[:, 0], mod[:, 1], mod[:, 2], mod[:, 3], mod[:, 4], mod[:, 5])
    ga = (2 * (ga >= 0) - 1) * jnp.maximum(jnp.abs(ga), 0.25)
    gb = (2 * (gb >= 0) - 1) * jnp.maximum(jnp.abs(gb), 0.25)
    h = _layernorm(x, axis=-1) * (1 + ca) + sa
    x = x + ga * _L0_attn_ref(h, L0_attn_W_in, L0_attn_W_x, L0_attn_W_dt, L0_attn_b_dt, L0_attn_gamma, L0_attn_beta)
    h = _layernorm(x, axis=-1) * (1 + cb) + sb
    x = x + gb * _L0_ffn_ref(h, L0_ffn_wqkv, L0_ffn_q_scale, L0_ffn_k_scale, L0_ffn_wo, L0_ffn_ln_g, L0_ffn_ln_b, L0_ffn_w1, L0_ffn_b1, L0_ffn_w2, L0_ffn_b2)
    return x

_drawn_inputs = setup_inputs


def setup_inputs(seed=0):
    import zlib

    import numpy as np

    out = dict(_drawn_inputs(seed))
    spreads = {'L0_attn_gamma': (1.0, 0.2),
     'L0_attn_beta': (0.0, 0.391),
     'L0_ffn_q_scale': (1.0, 0.6),
     'L0_ffn_k_scale': (1.0, 0.6),
     'L0_ffn_ln_g': (1.0, 0.6),
     'L0_ffn_ln_b': (0.0, 0.8),
     'L0_ffn_b1': (0.0, 0.8),
     'L0_ffn_b2': (0.0, 0.8)}
    factors = {'L0_attn_W_x': 4.225,
     'L0_attn_W_dt': 4.0,
     'L0_attn_b_dt': 8.0,
     'L0_ffn_wqkv': 7.256,
     'L0_ffn_wo': 7.293,
     'L0_ffn_w1': 8.0,
     'L0_ffn_w2': 8.0}
    for name, (base, spread) in spreads.items():
        noise = np.random.default_rng([zlib.crc32(name.encode()), seed]).standard_normal(out[name].shape)
        drawn = base * np.exp(spread * noise) if base else spread * noise
        out[name] = jnp.asarray(drawn.astype(out[name].dtype))
    for name, factor in factors.items():
        out[name] = (out[name] * factor).astype(out[name].dtype)
    return out
```

```python
from contextlib import ExitStack

import concourse.bass as bass
from concourse import mybir

ALU = mybir.AluOpType
ACT = mybir.ActivationFunctionType
F32 = mybir.dt.float32
F32R = mybir.dt.float32r
BF16 = mybir.dt.bfloat16
AX = mybir.AxisListType

D = 128
SEQS = 32
L = 256
TOK = SEQS * L
TILES = L // 128
DEPTH = 2
HEADS = 8
DH = 64
INNER = HEADS * DH
PAIRS = HEADS // 2
HID = 341
CHUNKS = [(0, 128), (128, 128), (256, HID - 256)]
WIN = 64
LN_EPS = 1e-5
STEP = 512
STEPS = TOK // STEP
LN2 = 0.6931471805599453
NORM_SHIFT = 20

ONCE = (
    "consts_in x_in mod_in consts_set silu_sig silu_done mod_mm mod_gate outer_mm outer_set "
    "w_in w_hi w_ready rot_ready o_comp o_st"
).split()
STEPPED = {
    "tensor": (
        "b_mean0 b_mean1 b_mean2 b_var0 b_var1 b_var2 b_xz b_dtmm "
        "q_proj0 q_proj1 v_proj0 v_proj1 qT_mm0 qT_mm1 kT_mm0 kT_mm1 "
        "s_mm0 s_mm1 pT_mm00 pT_mm01 pT_mm10 pT_mm11 oT_mm0 oT_mm1 wo_mm "
        "c_mean c_var c_up0 c_up1 c_up2 c_down").split(),
    "scalar": (
        "b_sq0 b_sq1 b_sq2 b_ln0 b_ln1 b_ln2 b_rstd0 b_rstd1 b_rstd2 b_tanh b_gate b_dt b_decay "
        "h_hi qk_sq0 qk_sq1 v_sb0 v_sb1 qk_ln0 qk_ln1 qk_r0 qk_r1 qT0 qT1 kT0 kT1 "
        "s_exp0 s_exp1 oT0 oT1 c_shift c_sq c_ln c_rstd c_hi c_gelu0 c_gelu1 c_gelu2").split(),
    "vector": (
        "b_dev0 b_dev1 b_dev2 b_xn0 b_xn1 b_xn2 b_h b_w b_scan b_g b_lng b_lnh b_x1 b_hB layer_done "
        "h_lo qk_ss0 qk_ss1 qk_clip0 qk_clip1 qk_n0 qk_n1 v_mix "
        "s_max0 s_max1 s_rec0 s_rec1 pT00 pT01 pT10 pT11 x_attn "
        "c_dev c_xn c_aff c_lo c_act0 c_act1 c_act2 x_ffn").split(),
    "gpsimd": "rot_u0 rot_u1 rot_w0 rot_w1 rot0 rot1 s_norm0 s_norm1".split(),
}


class Signals:

    def __init__(self, nc, ctx):
        names = ONCE + [n for group in STEPPED.values() for n in group]
        self.by_name = {n: ctx.enter_context(nc.semaphore(n)) for n in names}

    def __getitem__(self, name):
        return self.by_name[name]


def build(nc, xT, cT, wmod, w_inT, w_x0, w_dt, b_dt, gamma, beta, wqkv, q_scale, k_scale, wo,
          ln_g, ln_b, w1, b1, w2, b2, rot_tab, mask, ident_bf, ident, outT):
    with ExitStack() as ctx:
        def sb(name, shape, dt=F32):
            return ctx.enter_context(nc.sbuf_tensor(name, shape, dt))

        sig = Signals(nc, ctx)
        ps = ctx.enter_context(nc.psum_tensor("ps", [128, 8, 512], F32))
        PS_Q, PS_K, PS_V, PS_T, PS_S, PS_P, PS_C = 0, 1, 2, 3, 4, 6, 7

        X = sb("X", [128, TOK])
        X1 = sb("X1", [128, TOK])
        idf = sb("idf", [128, 128])
        idb = sb("idb", [128, 128], BF16)
        avg = sb("avg", [128, 128])
        maskb = sb("maskb", [128, TILES, 512], BF16)
        tab = sb("tab", [128, TILES, 4, DH])
        rot = sb("rot", [128, TILES, 4, DH])
        qks = sb("qks", [128, 2, DH])
        cTs = sb("cTs", [128, SEQS])
        csig = sb("csig", [128, SEQS])
        csilu = sb("csilu", [128, SEQS])
        wmods = sb("wmods", [128, 6 * D])
        mod = sb("mod", [128, 6, SEQS])
        gsgn = sb("gsgn", [128, 2, SEQS])
        gabs = sb("gabs", [128, 2, SEQS])
        winT = sb("winT", [128, 2 * D])
        wx = sb("wx", [1, D])
        wdt = sb("wdt", [1, D])
        wouter = sb("wouter", [128, D])
        vec = sb("vec", [128, 3])
        wq_raw = sb("wq_raw", [128, 3 * INNER])
        wq_hi = sb("wq_hi", [128, 3 * INNER], F32R)
        wq_lo = sb("wq_lo", [128, 3 * INNER], F32R)
        w1_raw = sb("w1_raw", [128, 2 * HID])
        w1_hi = sb("w1_hi", [128, 2 * HID], F32R)
        w1_lo = sb("w1_lo", [128, 2 * HID], F32R)
        wos = sb("wos", [128, PAIRS, D])
        w2s = sb("w2s", [128, 3, D])
        lvec = sb("lvec", [128, 3])
        b1s = sb("b1s", [128, 2, 3])
        h_hi = sb("h_hi_t", [128, L], F32R)
        h_lo = sb("h_lo_t", [128, L], F32R)
        qk_sq = sb("qk_sq", [128, 2 * INNER])
        ss = sb("ss", [128, TILES, 2 * HEADS])
        lnss = sb("lnss", [128, TILES, 2 * HEADS])
        rn = sb("rn", [128, TILES, 2 * HEADS])
        qk_n = sb("qk_n", [128, TILES, 2 * INNER])
        qk_u = sb("qk_u", [128, TILES, 2 * INNER])
        qk_w = sb("qk_w", [128, 2 * INNER])
        qT = sb("qT_t", [128, 2, PAIRS, L])
        kT = sb("kT_t", [128, 2, PAIRS, L])
        V = sb("V", [128, 2, TILES + 1, INNER])
        room = [qT[:, p, c:c + 2, :].rearrange("p c k -> p (c k)") for p in range(2) for c in (0, 2)]
        room += [kT[:, p, c:c + 2, :].rearrange("p c k -> p (c k)") for p in range(2) for c in (0, 2)]
        room += [V[:, p, t, :] for p in range(2) for t in range(3)]
        B = dict(zip("d sq ln r xn h tanh gate dt decay w y g".split(), room))
        nmax = sb("nmax", [128, TILES, HEADS])
        lsum = sb("lsum", [128, TILES, HEADS])
        lrec = sb("lrec", [128, TILES, HEADS])
        prob = sb("prob", [128, TILES, HEADS, 128])
        pT = sb("pT_t", [128, HEADS, 128])
        oT = sb("oT_t", [128, PAIRS, L])
        hs = sb("hs", [128, L])
        dev = sb("dev", [128, L])
        csq = sb("csq", [128, L])
        cln = sb("cln", [128, L])
        crstd = sb("crstd", [128, L])
        xn = sb("xn", [128, L])
        hn = sb("hn", [128, L])
        f_hi = sb("f_hi", [128, L], F32R)
        f_lo = sb("f_lo", [128, L], F32R)
        gel = sb("gel", [128, 3, L])
        act_ = sb("act_", [128, 3, L])
        biases = sb("biases", [128, 2])

        def heads(ap, n):
            return ap.rearrange("p (h d) -> p h d", h=n)

        def shifted(ap, col):
            return ((slice(0, 64), bass.ds(col, L), slice(0, L)),
                    (slice(64, 128), bass.ds(col, L - 1), slice(1, L)))

        def raise_once(eng, names):
            for name in names:
                eng.sem_inc(sig[name], 1)

        N_CONST = 12
        block = ctx.enter_context(nc.Block())

        def pipeline(eng, stages):
            with eng.Fori(0, DEPTH) as layer:
                base = eng.snap(layer * SEQS)
                stages["open"](eng, layer)

                def step(seq, par, first, do):
                    cnt = [eng.snap(base + (seq - k + 1)) if do[k] else None for k in range(3)]
                    cols = [eng.snap((seq - k) * L) if do[k] and not isinstance(seq, int)
                            else (seq - k) * L for k in range(3)]
                    st = [(cnt[k], cols[k], (par - k) % 2, seq - k) if do[k] else None for k in range(3)]
                    stages["step"](eng, *st)

                step(0, 0, True, (1, 0, 0))
                step(1, 1, False, (1, 1, 0))
                with eng.Fori(0, (SEQS - 2) // 2) as i:
                    for s in range(2):
                        step(eng.snap(i * 2 + (2 + s)), s, False, (1, 1, 1))
                step(SEQS, 0, False, (0, 1, 1))
                step(SEQS + 1, 1, False, (0, 0, 1))
                stages["close"](eng, layer)

        @block.sync
        def _(sp):
            for q in range(4):
                sp.dma_start(X1[:, q * (TOK // 4):(q + 1) * (TOK // 4)],
                             xT[:, q * (TOK // 4):(q + 1) * (TOK // 4)]).then_inc(sig["x_in"], 16)
            for dst, src in ((idf[:], ident), (idb[:], ident_bf), (maskb[:], mask),
                             (tab[:], rot_tab), (cTs[:], cT), (wmods[:], wmod), (winT[:], w_inT),
                             (wx[:], w_x0), (wdt[:], w_dt), (vec[:, 0:1], b_dt),
                             (vec[:, 1:2], gamma), (vec[:, 2:3], beta)):
                sp.dma_start(dst, src).then_inc(sig["consts_in"], 16)
            with sp.Fori(0, DEPTH) as layer:
                sp.wait_ge(sig["layer_done"], layer + 1)
                one = bass.ds(layer, 1)
                sp.dma_start(wq_raw[:], wqkv[one].rearrange("a p n -> (a p) n")).then_inc(sig["w_in"], 16)
                sp.dma_start(w1_raw[:], w1[one].rearrange("a p n -> (a p) n")).then_inc(sig["w_in"], 16)
                sp.dma_start(wos[:], wo[one].rearrange("a (c p) n -> p (a c) n", p=128)).then_inc(sig["w_in"], 16)
                for c, (lo, n) in enumerate(CHUNKS):
                    sp.dma_start(w2s[0:n, c, :], w2[one, lo:lo + n].rearrange("a p n -> (a p) n")).then_inc(sig["w_in"], 16)
                    for half in range(2):
                        sp.dma_start(b1s[0:n, half, c:c + 1],
                                     b1[one, half * HID + lo:half * HID + lo + n].rearrange("a p -> p a")
                                     ).then_inc(sig["w_in"], 16)
                sp.dma_start(qks[:, 0, :], q_scale[one].broadcast_to([128, DH])).then_inc(sig["w_in"], 16)
                sp.dma_start(qks[:, 1, :], k_scale[one].broadcast_to([128, DH])).then_inc(sig["w_in"], 16)
                for c, v in enumerate((ln_g, ln_b, b2)):
                    sp.dma_start(lvec[:, c:c + 1], v[one].rearrange("a p -> p a")).then_inc(sig["w_in"], 16)
            for b in range(SEQS):
                sp.wait_ge(sig["o_comp"], b + 1)
                sp.dma_start(outT[:, b * L:(b + 1) * L], X1[:, b * L:(b + 1) * L]).then_inc(sig["o_st"], 16)
            sp.wait_ge(sig["o_st"], 16 * SEQS)

        W_LOADS = 3 + 3 * 3 + 2 + 3

        def pe_open(pe, layer):
            pe.wait_ge(sig["w_ready"], layer + 1)
            pe.wait_ge(sig["w_in"], (layer + 1) * (16 * W_LOADS))

        def pe_close(pe, layer):
            pass

        def pe_step(pe, A, Bs, C):
            mm = nc.tensor.matmul

            def scores(t):
                n, _, par, _ = Bs
                if t == 0:
                    pe.wait_ge(sig["qT1"], n + 1)
                    pe.wait_ge(sig["kT1"], n + 1)
                    pe.wait_ge(sig["s_exp1"], n)
                else:
                    pe.wait_ge(sig["s_exp0"], n + 1)
                for r in range(2):
                    mm(ps[:, PS_S + r, :], idb[:], maskb[:, t, :], start=True, stop=True)
                last = None
                for c in range(PAIRS):
                    for r in range(2):
                        rows = slice(64 * r, 64 * r + 64)
                        o = slice(128 * c, 128 * c + 128)
                        if t == 0:
                            last = mm(ps[:, PS_S + r, o], qT[rows, par, c, 0:128], kT[rows, par, c, 0:128],
                                      start=False, stop=True, skip_group_check=True)
                        else:
                            back = kT[rows, par, c, 64:192].rearrange("p (w k) -> p w k", w=2)[:, ::-1, :]
                            mm(ps[0:64, PS_S + r, o].rearrange("p (w k) -> p w k", w=2),
                               qT[rows, par, c, 128:192], back, start=False, stop=True, skip_group_check=True)
                            last = mm(ps[64:128, PS_S + r, o], qT[rows, par, c, 192:256],
                                      kT[rows, par, c, 128:256], start=False, stop=True, skip_group_check=True)
                last.then_inc(sig[f"s_mm{t}"], 1)

            def project(t):
                n = A[0]
                if t == 0:
                    pe.wait_ge(sig["h_hi"], n + 1)
                    pe.wait_ge(sig["h_lo"], n + 1)
                    pe.wait_ge(sig["qk_n1"], n)
                    pe.wait_ge(sig["kT1"], n)
                else:
                    pe.wait_ge(sig["qk_n0"], n + 1)
                tok = slice(128 * t, 128 * t + 128)
                for bank in range(3):
                    if bank == 2 and t == 1:
                        pe.wait_ge(sig["v_sb0"], n + 1)
                    o = slice(INNER * bank, INNER * bank + INNER)
                    mm(ps[:, PS_Q + bank, :], h_hi[:, tok], wq_lo[:, o], start=True, stop=False)
                    mm(ps[:, PS_Q + bank, :], h_lo[:, tok], wq_hi[:, o], start=False, stop=False)
                    last = mm(ps[:, PS_Q + bank, :], h_hi[:, tok], wq_hi[:, o], start=False, stop=True)
                    if bank == 1:
                        last.then_inc(sig[f"q_proj{t}"], 1)
                last.then_inc(sig[f"v_proj{t}"], 1)

            def transposes(t):
                n = A[0]
                pe.wait_ge(sig[f"rot{t}"], n + 1)
                if Bs:
                    pe.wait_ge(sig[f"oT{t}"], Bs[0] + 1)
                else:
                    pe.wait_ge(sig["oT1"], n)
                if t == 1:
                    pe.wait_ge(sig["qT0"], n + 1)
                for c in range(PAIRS):
                    last = nc.tensor.transpose(ps[:, PS_T, 128 * c:128 * c + 128],
                                               qk_u[:, t, 128 * c:128 * c + 128], idf[:])
                last.then_inc(sig[f"qT_mm{t}"], 1)
                if t == 0:
                    pe.wait_ge(sig["v_sb1"], n + 1)
                else:
                    pe.wait_ge(sig["kT0"], n + 1)
                for c in range(PAIRS):
                    last = nc.tensor.transpose(ps[:, PS_V, 128 * c:128 * c + 128],
                                               qk_u[:, t, INNER + 128 * c:INNER + 128 * c + 128], idf[:])
                last.then_inc(sig[f"kT_mm{t}"], 1)

            def prob_transposes(t, half):
                n = Bs[0]
                if half == 0:
                    pe.wait_ge(sig[f"s_norm{t}"], n + 1)
                if (t, half) == (0, 0):
                    pe.wait_ge(sig["pT11"], n)
                else:
                    before = {(0, 1): "pT00", (1, 0): "pT01", (1, 1): "pT10"}[(t, half)]
                    pe.wait_ge(sig[before], n + 1)
                for j in range(4):
                    c, r = 2 * half + j // 2, j % 2
                    last = nc.tensor.transpose(ps[:, PS_P, 128 * j:128 * j + 128],
                                               prob[:, t, 4 * r + c, :], idf[:])
                last.then_inc(sig[f"pT_mm{t}{half}"], 1)

            def attend(t):
                n, _, par, _ = Bs
                if t == 0:
                    pe.wait_ge(sig["qT1"], n + 1)
                    pe.wait_ge(sig["v_mix"], n + 1)
                elif A:
                    pe.wait_ge(sig["qT0"], A[0] + 1)
                else:
                    pe.wait_ge(sig["oT0"], n + 1)
                for half in range(2):
                    pe.wait_ge(sig[f"pT{t}{half}"], n + 1)
                    for j in range(4):
                        c, r = 2 * half + j // 2, j % 2
                        h = 2 * c + r
                        rows = slice(64 * r, 64 * r + 64)
                        feat = slice(DH * h, DH * h + DH)
                        if t == 0:
                            last = mm(ps[rows, PS_T, 128 * c:128 * c + 128], V[:, par, 0, feat],
                                      pT[:, 2 * c + r, :], start=True, stop=True)
                        else:
                            mm(ps[rows, PS_T, 128 * c:128 * c + 64], V[:, par, TILES, feat],
                               pT[:, 2 * c + r, 0:64], start=True, stop=True)
                            last = mm(ps[rows, PS_T, 128 * c + 64:128 * c + 128], V[:, par, 1, feat],
                                      pT[:, 2 * c + r, 64:128], start=True, stop=True)
                last.then_inc(sig[f"oT_mm{t}"], 1)

            def out_proj():
                n = Bs[0]
                pe.wait_ge(sig["oT1"], n + 1)
                if C:
                    pe.wait_ge(sig["x_ffn"], C[0] + 1)
                else:
                    pe.wait_ge(sig["x_ffn"], n)
                for c in range(PAIRS):
                    last = mm(ps[:, PS_C, 0:L], wos[:, c, :], oT[:, c, :], start=(c == 0), stop=(c == PAIRS - 1))
                last.then_inc(sig["wo_mm"], 1)

            def c_mean():
                n = C[0]
                pe.wait_ge(sig["c_shift"], n + 1)
                pe.wait_ge(sig["x_attn"], n + 1)
                if Bs:
                    pe.wait_ge(sig["x_attn"], Bs[0])
                mm(ps[:, PS_C, 0:L], avg[:], hs[:], start=True, stop=True).then_inc(sig["c_mean"], 1)

            def c_var():
                pe.wait_ge(sig["c_sq"], C[0] + 1)
                mm(ps[:, PS_C, 0:L], avg[:], csq[:], start=True, stop=True).then_inc(sig["c_var"], 1)

            def c_up(k):
                n = C[0]
                if k == 0:
                    pe.wait_ge(sig["c_lo"], n + 1)
                else:
                    pe.wait_ge(sig[f"c_act{k - 1}"], n + 1)
                lo, m = CHUNKS[k]
                for half in (1, 0):
                    o = slice(half * HID + lo, half * HID + lo + m)
                    dst = ps[0:m, PS_C, (1 - half) * L:(1 - half) * L + L]
                    mm(dst, w1_lo[:, o], f_hi[:], start=True, stop=False)
                    mm(dst, w1_hi[:, o], f_lo[:], start=False, stop=False)
                    last = mm(dst, w1_hi[:, o], f_hi[:], start=False, stop=True)
                last.then_inc(sig[f"c_up{k}"], 1)

            def c_down():
                n = C[0]
                pe.wait_ge(sig["c_act2"], n + 1)
                for k, (lo, m) in enumerate(CHUNKS):
                    last = mm(ps[:, PS_C, 0:L], w2s[0:m, k, :], act_[0:m, k, :], start=(k == 0), stop=(k == 2))
                last.then_inc(sig["c_down"], 1)

            if Bs: scores(0)
            if C: c_mean()
            if A: project(0)
            if C: c_var()
            if Bs: scores(1)
            if Bs: prob_transposes(0, 0)
            if Bs: prob_transposes(0, 1)
            if A: project(1)
            if Bs: attend(0)
            if A: transposes(0)
            if C: c_up(0)
            if Bs: prob_transposes(1, 0)
            if C: c_up(1)
            if Bs: prob_transposes(1, 1)
            if C: c_up(2)
            if Bs: attend(1)
            if C: c_down()
            if Bs: out_proj()
            if A: transposes(1)

        @block.tensor
        def _(pe):
            raise_once(pe, STEPPED["tensor"])
            mm = nc.tensor.matmul
            pe.wait_ge(sig["silu_done"], 1)
            pe.wait_ge(sig["consts_in"], 16 * N_CONST)
            for j in range(6):
                last = mm(ps[:, 0, SEQS * j:SEQS * (j + 1)], wmods[:, D * j:D * (j + 1)], csilu[:],
                          start=True, stop=True)
            last.then_inc(sig["mod_mm"], 1)
            mm(ps[:, 1, 0:D], wx[:], wdt[:], start=True, stop=True).then_inc(sig["outer_mm"], 1)
            pe.wait_ge(sig["outer_set"], 1)
            pe.wait_ge(sig["mod_gate"], 1)
            pe.wait_ge(sig["consts_set"], 1)
            pe.wait_ge(sig["x_in"], 64)
            with pe.Fori(0, STEPS) as i:
                n = pe.snap(i + 2)
                for k in range(3):
                    if k == 0:
                        rhs = X1[:, bass.ds(i * STEP, STEP)]
                    elif k == 1:
                        pe.wait_ge(sig["b_g"], n)
                        rhs = B["g"]
                    else:
                        pe.wait_ge(sig["b_x1"], n)
                        rhs = X1[:, bass.ds(i * STEP, STEP)]
                    if k == 0:
                        pe.wait_ge(sig["b_dev2"], n - 1)
                    mm(ps[:, 0, :], avg[:], rhs, start=True, stop=True).then_inc(sig[f"b_mean{k}"], 1)
                    pe.wait_ge(sig[f"b_sq{k}"], n)
                    if k == 0:
                        pe.wait_ge(sig["b_ln2"], n - 1)
                    mm(ps[:, 1, :], avg[:], B["sq"], start=True, stop=True).then_inc(sig[f"b_var{k}"], 1)
                    if k == 0:
                        pe.wait_ge(sig["b_h"], n)
                        for half in range(2):
                            last = mm(ps[:, 2 + half, :], winT[:, D * half:D * half + D], B["h"],
                                      start=True, stop=True)
                        last.then_inc(sig["b_xz"], 1)
                        pe.wait_ge(sig["b_tanh"], n)
                        mm(ps[:, 4, :], wouter[:], B["tanh"], start=True, stop=True).then_inc(sig["b_dtmm"], 1)
            pipeline(pe, {"open": pe_open, "close": pe_close, "step": pe_step})

        def act_open(act, layer):
            act.wait_ge(sig["w_in"], (layer + 1) * (16 * W_LOADS))

        def act_step(act, A, Bs, C):
            f = nc.scalar.activation

            def h_high():
                n, col, _, _ = A
                act.wait_ge(sig["v_proj1"], n)
                act.wait_ge(sig["h_lo"], n)
                for rows, src, dst in shifted(X, col):
                    last = f(h_hi[rows, dst], X[rows, src], ACT.Copy)
                last.then_inc(sig["h_hi"], 1)

            def exps(t):
                n = Bs[0]
                act.wait_ge(sig[f"s_max{t}"], n + 1)
                act.wait_ge(sig[f"pT_mm{t}1"], n)
                act.wait_ge(sig[f"s_rec{t}"], n)
                for h in range(HEADS):
                    last = f(prob[:, t, h, :], ps[:, PS_S + h // 4, 128 * (h % 4):128 * (h % 4) + 128], ACT.Exp,
                             bias=nmax[:, t, h:h + 1], accum_out=lsum[:, t, h:h + 1])
                last.then_inc(sig[f"s_exp{t}"], 1)

            def squares(t):
                n = A[0]
                act.wait_ge(sig[f"q_proj{t}"], n + 1)
                act.wait_ge(sig["qk_ss0"] if t else sig["qk_ss1"], n + t)
                f(heads(qk_sq[:], 2), ps[:, PS_Q:PS_Q + 2, :], ACT.Square).then_inc(sig[f"qk_sq{t}"], 1)

            def values(t):
                n, _, par, _ = A
                act.wait_ge(sig[f"v_proj{t}"], n + 1)
                f(V[:, par, t, :], ps[:, PS_V, :], ACT.Copy).then_inc(sig[f"v_sb{t}"], 1)

            def norms(t):
                n = A[0]
                act.wait_ge(sig[f"qk_clip{t}"], n + 1)
                f(lnss[:, t, :], ss[:, t, :], ACT.Ln, scale=float(2 ** NORM_SHIFT)).then_inc(sig[f"qk_ln{t}"], 1)
                act.wait_ge(sig[f"qk_ln{t}"], n + 1)
                act.wait_ge(sig[f"qk_n{t}"], n)
                f(rn[:, t, :], lnss[:, t, :], ACT.Exp, scale=-0.5, bias=biases[:, 1:2]).then_inc(sig[f"qk_r{t}"], 1)

            def shift():
                n, col, _, _ = C
                act.wait_ge(sig["x_attn"], n + 1)
                act.wait_ge(sig["c_dev"], n)
                for rows, src, dst in shifted(X, col):
                    last = f(hs[rows, dst], X[rows, src], ACT.Copy)
                last.then_inc(sig["c_shift"], 1)

            def c_square():
                n = C[0]
                act.wait_ge(sig["c_dev"], n + 1)
                f(csq[:], dev[:], ACT.Square).then_inc(sig["c_sq"], 1)

            def c_norm():
                n = C[0]
                act.wait_ge(sig["c_var"], n + 1)
                f(cln[:], ps[:, PS_C, 0:L], ACT.Ln, bias=biases[:, 0:1]).then_inc(sig["c_ln"], 1)
                act.wait_ge(sig["c_ln"], n + 1)
                act.wait_ge(sig["c_xn"], n)
                f(crstd[:], cln[:], ACT.Exp, scale=-0.5).then_inc(sig["c_rstd"], 1)

            def c_high():
                n = C[0]
                act.wait_ge(sig["c_aff"], n + 1)
                act.wait_ge(sig["c_up2"], n)
                f(f_hi[:], hn[:], ACT.Copy).then_inc(sig["c_hi"], 1)

            def gelu(k):
                n = C[0]
                m = CHUNKS[k][1]
                act.wait_ge(sig[f"c_up{k}"], n + 1)
                f(gel[0:m, k, :], ps[0:m, PS_C, 0:L], ACT.Gelu, bias=b1s[0:m, 1, k:k + 1]).then_inc(sig[f"c_gelu{k}"], 1)

            def attended(t):
                n = Bs[0]
                act.wait_ge(sig[f"oT_mm{t}"], n + 1)
                if t == 0:
                    act.wait_ge(sig["wo_mm"], n)
                f(oT[:, :, 128 * t:128 * t + 128], ps[:, PS_T, :].rearrange("p (c k) -> p c k", c=PAIRS),
                  ACT.Copy).then_inc(sig[f"oT{t}"], 1)

            def rotated(t):
                n, _, par, _ = A
                for name, dst, bank in (("qT", qT, PS_T), ("kT", kT, PS_V)):
                    act.wait_ge(sig[f"{name}_mm{t}"], n + 1)
                    f(dst[:, par, :, 128 * t:128 * t + 128], ps[:, bank, :].rearrange("p (c k) -> p c k", c=PAIRS),
                      ACT.Copy).then_inc(sig[f"{name}{t}"], 1)

            if A:
                if Bs: act.wait_ge(sig["x_attn"], Bs[0])
                h_high()
            if C: shift()
            if Bs: exps(0)
            if C: c_square()
            if A: squares(0)
            if A: values(0)
            if C: c_norm()
            if Bs: exps(1)
            if A: norms(0)
            if A: squares(1)
            if A: values(1)
            if C: c_high()
            if A: norms(1)
            if Bs: attended(0)
            if A: rotated(0)
            if C: gelu(0)
            if C: gelu(1)
            if C: gelu(2)
            if Bs: attended(1)
            if A: rotated(1)

        @block.scalar
        def _(act):
            raise_once(act, STEPPED["scalar"])
            f = nc.scalar.activation
            act.wait_ge(sig["consts_in"], 16 * N_CONST)
            f(csig[:], cTs[:], ACT.Sigmoid).then_inc(sig["silu_sig"], 1)
            act.wait_ge(sig["consts_set"], 1)
            with act.Fori(0, STEPS) as i:
                n = act.snap(i + 2)

                def ln_stats(k):
                    act.wait_ge(sig[f"b_dev{k}"], n)
                    f(B["sq"], B["d"], ACT.Square).then_inc(sig[f"b_sq{k}"], 1)
                    act.wait_ge(sig[f"b_var{k}"], n)
                    f(B["ln"], ps[:, 1, :], ACT.Ln, bias=biases[:, 0:1]).then_inc(sig[f"b_ln{k}"], 1)
                    act.wait_ge(sig[f"b_ln{k}"], n)
                    f(B["r"], B["ln"], ACT.Exp, scale=-0.5).then_inc(sig[f"b_rstd{k}"], 1)

                ln_stats(0)
                act.wait_ge(sig["b_xz"], n)
                f(B["tanh"], ps[:, 2, :], ACT.Tanh).then_inc(sig["b_tanh"], 1)
                f(B["gate"], ps[:, 3, :], ACT.Sigmoid).then_inc(sig["b_gate"], 1)
                act.wait_ge(sig["b_dtmm"], n)
                f(B["dt"], ps[:, 4, :], ACT.Sigmoid, bias=vec[:, 0:1]).then_inc(sig["b_dt"], 1)
                act.wait_ge(sig["b_dt"], n)
                f(B["decay"], B["dt"], ACT.Sigmoid, scale=-1.0).then_inc(sig["b_decay"], 1)
                ln_stats(1)
                ln_stats(2)
            pipeline(act, {"open": act_open, "close": lambda e, l: None, "step": act_step})

        def dve_open(dve, layer):
            v = nc.vector
            dve.wait_ge(sig["w_in"], (layer + 1) * (16 * W_LOADS))
            dve.wait_ge(sig["layer_done"], layer + 1)
            v.tensor_copy(wq_hi[:], wq_raw[:])
            v.tensor_copy(w1_hi[:], w1_raw[:]).then_inc(sig["w_hi"], 1)
            dve.wait_ge(sig["w_hi"], layer + 1)
            v.tensor_tensor(wq_lo[:], wq_raw[:], wq_hi[:].bitcast(F32), ALU.subtract)
            v.tensor_tensor(w1_lo[:], w1_raw[:], w1_hi[:].bitcast(F32), ALU.subtract).then_inc(sig["w_ready"], 1)
            for t in range(TILES):
                v.tensor_tensor(rot[:, t, 0:2, :], tab[:, t, 0:2, :], qks[:], ALU.mult)
                for j in range(2):
                    last = v.tensor_tensor(heads(rot[:, t, 2 + j, :], 2), heads(tab[:, t, 2 + j, :], 2),
                                           heads(qks[:, j, :], 2)[:, ::-1, :], ALU.mult)
            last.then_inc(sig["rot_ready"], 1)

        def dve_close(dve, layer):
            dve.wait_ge(sig["x_ffn"], layer * SEQS + (SEQS + 1))
            nc.vector.tensor_copy(biases[:, 1:2], biases[:, 1:2]).then_inc(sig["layer_done"], 1)

        def dve_step(dve, A, Bs, C):
            v = nc.vector

            def h_low():
                n, col, _, _ = A
                dve.wait_ge(sig["h_hi"], n + 1)
                dve.wait_ge(sig["v_proj1"], n)
                for rows, src, dst in shifted(X, col):
                    last = v.tensor_tensor(h_lo[rows, dst], X[rows, src], h_hi[rows, dst].bitcast(F32), ALU.subtract)
                last.then_inc(sig["h_lo"], 1)

            def maxes(t):
                n = Bs[0]
                dve.wait_ge(sig[f"s_mm{t}"], n + 1)
                dve.wait_ge(sig[f"s_exp{t}"], n)
                v.tensor_reduce(nmax[:, t, :], ps[:, PS_S:PS_S + 2, :].rearrange("p b (c k) -> p (b c) k", c=4),
                                AX.X, ALU.max, negate=True).then_inc(sig[f"s_max{t}"], 1)

            def sums(t):
                n = Bs[0]
                dve.wait_ge(sig[f"s_exp{t}"], n + 1)
                dve.wait_ge(sig[f"s_norm{t}"], n)
                v.reciprocal(lrec[:, t, :], lsum[:, t, :]).then_inc(sig[f"s_rec{t}"], 1)

            def square_sums(t):
                n = A[0]
                dve.wait_ge(sig[f"qk_sq{t}"], n + 1)
                dve.wait_ge(sig[f"qk_ln{t}"], n)
                v.tensor_reduce(ss[:, t, :], heads(qk_sq[:], 2 * HEADS), AX.X, ALU.add).then_inc(sig[f"qk_ss{t}"], 1)
                dve.wait_ge(sig[f"qk_ss{t}"], n + 1)
                v.tensor_scalar(ss[:, t, :], ss[:, t, :], 1e-24, None, ALU.max).then_inc(sig[f"qk_clip{t}"], 1)

            def normed(t):
                n = A[0]
                dve.wait_ge(sig[f"qk_r{t}"], n + 1)
                dve.wait_ge(sig[f"rot_w{t}"], n)
                v.tensor_tensor(heads(qk_n[:, t, :], 2 * HEADS),
                                ps[:, PS_Q:PS_Q + 2, :].rearrange("p b (h d) -> p (b h) d", h=HEADS),
                                rn[:, t, :].unsqueeze(2).broadcast_to([128, 2 * HEADS, DH]),
                                ALU.mult).then_inc(sig[f"qk_n{t}"], 1)

            def mixed():
                n, _, par, _ = A
                dve.wait_ge(sig["v_sb1"], n + 1)
                v.tensor_copy(V[0:64, par, TILES, :], V[0:64, par, 1, :])
                v.tensor_copy(V[64:128, par, TILES, :], V[64:128, par, 0, :]).then_inc(sig["v_mix"], 1)

            def prob_copy(t, half):
                n = Bs[0]
                dve.wait_ge(sig[f"pT_mm{t}{half}"], n + 1)
                if t == 0:
                    dve.wait_ge(sig["oT_mm1"], n)
                else:
                    dve.wait_ge(sig["oT_mm0"], n + 1)
                v.tensor_copy(pT[:, 4 * half:4 * half + 4, :],
                              ps[:, PS_P, :].rearrange("p (j k) -> p j k", j=4)).then_inc(sig[f"pT{t}{half}"], 1)

            def residual_attn():
                n, col, _, _ = Bs
                dve.wait_ge(sig["wo_mm"], n + 1)
                v.tensor_tensor(X[:, bass.ds(col, L)], ps[:, PS_C, 0:L], X[:, bass.ds(col, L)],
                                ALU.add).then_inc(sig["x_attn"], 1)

            def c_dev():
                n = C[0]
                dve.wait_ge(sig["c_mean"], n + 1)
                dve.wait_ge(sig["c_xn"], n)
                v.tensor_tensor(dev[:], hs[:], ps[:, PS_C, 0:L], ALU.subtract).then_inc(sig["c_dev"], 1)

            def c_apply():
                n = C[0]
                dve.wait_ge(sig["c_rstd"], n + 1)
                dve.wait_ge(sig["c_aff"], n)
                v.tensor_tensor(xn[:], dev[:], crstd[:], ALU.mult).then_inc(sig["c_xn"], 1)
                dve.wait_ge(sig["c_xn"], n + 1)
                dve.wait_ge(sig["c_lo"], n)
                v.tensor_scalar(hn[:], xn[:], lvec[:, 0:1], lvec[:, 1:2], ALU.mult, ALU.add).then_inc(sig["c_aff"], 1)

            def c_low():
                n = C[0]
                dve.wait_ge(sig["c_hi"], n + 1)
                dve.wait_ge(sig["c_up2"], n)
                v.tensor_tensor(f_lo[:], hn[:], f_hi[:].bitcast(F32), ALU.subtract).then_inc(sig["c_lo"], 1)

            def geglu(k):
                n = C[0]
                m = CHUNKS[k][1]
                dve.wait_ge(sig[f"c_gelu{k}"], n + 1)
                dve.wait_ge(sig["c_down"], n)
                v.scalar_tensor_tensor(act_[0:m, k, :], ps[0:m, PS_C, L:2 * L], b1s[0:m, 0, k:k + 1],
                                       gel[0:m, k, :], ALU.add, ALU.mult).then_inc(sig[f"c_act{k}"], 1)

            def residual_ffn():
                n, col, _, _ = C
                dve.wait_ge(sig["c_down"], n + 1)
                v.scalar_tensor_tensor(X[:, bass.ds(col, L)], ps[:, PS_C, 0:L], lvec[:, 2:3],
                                       X[:, bass.ds(col, L)], ALU.add, ALU.add).then_inc(sig["x_ffn"], 1)

            if A: h_low()
            if Bs: maxes(0)
            if C: c_dev()
            if A: square_sums(0)
            if Bs: sums(0)
            if Bs: maxes(1)
            if C: c_apply()
            if A: normed(0)
            if Bs: prob_copy(0, 0)
            if Bs: prob_copy(0, 1)
            if Bs: sums(1)
            if A: square_sums(1)
            if C: c_low()
            if A: mixed()
            if A: normed(1)
            if C: geglu(0)
            if Bs: prob_copy(1, 0)
            if C: geglu(1)
            if Bs: prob_copy(1, 1)
            if C: geglu(2)
            if C: residual_ffn()
            if Bs: residual_attn()

        @block.vector
        def _(dve):
            raise_once(dve, STEPPED["vector"])
            v = nc.vector
            v.memset(avg[:], 1.0 / D)
            v.memset(biases[:, 0:1], LN_EPS)
            v.memset(biases[:, 1:2], NORM_SHIFT / 2 * LN2)
            v.memset(h_hi[64:128, 0:1].bitcast(F32), 0.0)
            v.memset(h_lo[64:128, 0:1].bitcast(F32), 0.0)
            v.memset(hs[64:128, 0:1], 0.0).then_inc(sig["consts_set"], 1)
            dve.wait_ge(sig["silu_sig"], 1)
            v.tensor_tensor(csilu[:], cTs[:], csig[:], ALU.mult).then_inc(sig["silu_done"], 1)
            dve.wait_ge(sig["mod_mm"], 1)
            modp = ps[:, 0, 0:6 * SEQS].rearrange("p (j b) -> p j b", j=6)
            for j in range(6):
                v.tensor_scalar(mod[:, j, :], modp[:, j, :], 1.0 if j in (1, 4) else 0.0, None, ALU.add)
            dve.wait_ge(sig["outer_mm"], 1)
            v.tensor_copy(wouter[:], ps[:, 1, 0:D]).then_inc(sig["outer_set"], 1)
            for s, j in enumerate((2, 5)):
                last = v.tensor_scalar(gsgn[:, s, :], modp[:, j, :], 0.0, 2.0, ALU.is_ge, ALU.mult)
            last.then_inc(sig["mod_in"], 1)
            dve.wait_ge(sig["mod_in"], 1)
            for s, j in enumerate((2, 5)):
                last = v.scalar_tensor_tensor(gabs[:, s, :], modp[:, j, :], -1.0, mod[:, j, :], ALU.mult, ALU.max)
            last.then_inc(sig["mod_in"], 1)
            dve.wait_ge(sig["mod_in"], 2)
            v.tensor_scalar(gabs[:], gabs[:], 0.25, None, ALU.max).then_inc(sig["mod_in"], 1)
            dve.wait_ge(sig["mod_in"], 3)
            for s, j in enumerate((2, 5)):
                last = v.scalar_tensor_tensor(mod[:, j, :], gsgn[:, s, :], -1.0, gabs[:, s, :], ALU.add, ALU.mult)
            last.then_inc(sig["mod_gate"], 1)
            dve.wait_ge(sig["mod_gate"], 1)
            dve.wait_ge(sig["x_in"], 64)
            with dve.Fori(0, STEPS) as i:
                n = dve.snap(i + 2)
                col = dve.snap(i * STEP)
                seq = dve.snap(i * 2)

                def deviation(k, src):
                    dve.wait_ge(sig[f"b_mean{k}"], n)
                    v.tensor_tensor(B["d"], src, ps[:, 0, :], ALU.subtract).then_inc(sig[f"b_dev{k}"], 1)
                    dve.wait_ge(sig[f"b_rstd{k}"], n)
                    v.tensor_tensor(B["xn"], B["d"], B["r"], ALU.mult).then_inc(sig[f"b_xn{k}"], 1)
                    dve.wait_ge(sig[f"b_xn{k}"], n)

                x_now = X1[:, bass.ds(col, STEP)]
                deviation(0, x_now)
                for b in range(2):
                    o = slice(L * b, L * b + L)
                    last = v.tensor_scalar(B["h"][:, o], B["xn"][:, o], mod[:, 1, bass.ds(seq + b, 1)],
                                           mod[:, 0, bass.ds(seq + b, 1)], ALU.mult, ALU.add)
                last.then_inc(sig["b_h"], 1)
                dve.wait_ge(sig["b_decay"], n)
                v.scalar_tensor_tensor(B["w"], B["decay"], -1.0, B["tanh"], ALU.add, ALU.mult).then_inc(sig["b_w"], 1)
                dve.wait_ge(sig["b_w"], n)
                for b in range(2):
                    o = slice(L * b, L * b + L)
                    last = v.tensor_tensor_scan(B["y"][:, o], B["decay"][:, o], B["w"][:, o], 0.0, ALU.mult, ALU.subtract)
                last.then_inc(sig["b_scan"], 1)
                dve.wait_ge(sig["b_scan"], n)
                v.tensor_tensor(B["g"], B["y"], B["gate"], ALU.mult).then_inc(sig["b_g"], 1)
                dve.wait_ge(sig["b_g"], n)
                deviation(1, B["g"])
                v.tensor_scalar(B["w"], B["xn"], vec[:, 1:2], vec[:, 2:3], ALU.mult, ALU.add).then_inc(sig["b_lng"], 1)
                dve.wait_ge(sig["b_lng"], n)
                v.tensor_tensor(B["y"], B["w"], B["h"], ALU.add).then_inc(sig["b_lnh"], 1)
                dve.wait_ge(sig["b_lnh"], n)
                for b in range(2):
                    o = slice(L * b, L * b + L)
                    xs = X1[:, bass.ds(col + L * b, L)]
                    last = v.scalar_tensor_tensor(xs, B["y"][:, o], mod[:, 2, bass.ds(seq + b, 1)], xs, ALU.mult, ALU.add)
                last.then_inc(sig["b_x1"], 1)
                dve.wait_ge(sig["b_x1"], n)
                deviation(2, x_now)
                for b in range(2):
                    o = slice(L * b, L * b + L)
                    last = v.tensor_scalar(X[:, bass.ds(col + L * b, L)], B["xn"][:, o], mod[:, 4, bass.ds(seq + b, 1)],
                                           mod[:, 3, bass.ds(seq + b, 1)], ALU.mult, ALU.add)
                last.then_inc(sig["b_hB"], 1)
            dve.wait_ge(sig["b_hB"], STEPS + 1)
            pipeline(dve, {"open": dve_open, "close": dve_close, "step": dve_step})
            for b in range(SEQS):
                o = slice(L * b, L * b + L)
                v.scalar_tensor_tensor(X1[:, o], X[:, o], mod[:, 5, b:b + 1], X1[:, o], ALU.mult,
                                       ALU.add).then_inc(sig["o_comp"], 1)

        def pool_open(pool, layer):
            pool.wait_ge(sig["rot_ready"], layer + 1)

        def pool_step(pool, A, Bs, C):
            g = nc.gpsimd

            def normalise(t):
                n = Bs[0]
                pool.wait_ge(sig[f"s_rec{t}"], n + 1)
                g.tensor_tensor(prob[:, t], prob[:, t], lrec[:, t, :].unsqueeze(2).broadcast_to([128, HEADS, 128]),
                                ALU.mult).then_inc(sig[f"s_norm{t}"], 1)

            def rotate(t):
                n = A[0]
                pool.wait_ge(sig[f"qk_n{t}"], n + 1)
                pool.wait_ge(sig[f"kT_mm{t}"], n)
                for j in range(2):
                    o = slice(INNER * j, INNER * j + INNER)
                    last = g.tensor_tensor(heads(qk_u[:, t, o], HEADS), heads(qk_n[:, t, o], HEADS),
                                           rot[:, t, j, :].unsqueeze(1).broadcast_to([128, HEADS, DH]), ALU.mult)
                last.then_inc(sig[f"rot_u{t}"], 1)
                pool.wait_ge(sig["rot0"] if t else sig["rot1"], n + t)
                for j in range(2):
                    o = slice(INNER * j, INNER * j + INNER)
                    for half in range(2):
                        a, b = slice(32 * half, 32 * half + 32), slice(32 - 32 * half, 64 - 32 * half)
                        last = g.tensor_tensor(heads(qk_w[:, o], HEADS)[:, :, a], heads(qk_n[:, t, o], HEADS)[:, :, b],
                                               rot[:, t, 2 + j, a].unsqueeze(1).broadcast_to([128, HEADS, 32]), ALU.mult)
                last.then_inc(sig[f"rot_w{t}"], 1)
                pool.wait_ge(sig[f"rot_u{t}"], n + 1)
                pool.wait_ge(sig[f"rot_w{t}"], n + 1)
                g.tensor_tensor(qk_u[:, t, :], qk_u[:, t, :], qk_w[:], ALU.add).then_inc(sig[f"rot{t}"], 1)

            if Bs: normalise(0)
            if A: rotate(0)
            if Bs: normalise(1)
            if A: rotate(1)

        @block.gpsimd
        def _(pool):
            raise_once(pool, STEPPED["gpsimd"])
            pipeline(pool, {"open": pool_open, "close": lambda e, l: None, "step": pool_step})


def kernel(**inputs):
    import numpy as np
    import ml_dtypes
    import concourse.bacc as bacc
    from concourse.bass_utils import run_bass_kernel_spmd

    def t(name):
        return np.asarray(inputs[name])

    half = np.arange(0, DH, 2, dtype=np.float32)
    freqs = np.arange(L, dtype=np.float32)[:, None] * (1.0 / 10000.0 ** (half / DH)).astype(np.float32)[None, :]
    base = (half + 0.4 * DH) / (1.4 * DH)
    scale = base[None, :] ** ((np.arange(L) - L // 2) / float(WIN // 2))[:, None]
    cos, sin, scale = (np.concatenate([a, a], -1) for a in (np.cos(freqs), np.sin(freqs), scale))
    sin = sin * np.where(np.arange(DH) < DH // 2, -1.0, 1.0)[None, :]
    rot_tab = np.stack([8.0 * cos * scale, cos / scale, 8.0 * sin * scale, sin / scale], 1).astype(np.float32)
    rot_tab = rot_tab.reshape(TILES, 128, 4, DH).transpose(1, 0, 2, 3)
    row, slot = np.arange(128)[:, None], np.arange(128)[None, :]
    keys = np.stack([np.broadcast_to(slot, (128, 128)),
                     np.where((row < 64) & (slot >= 64), slot, slot + 128)])
    query = np.stack([np.broadcast_to(row, (128, 128)), np.broadcast_to(row + 128, (128, 128))])
    seen = (keys <= query) & (query <= keys + WIN)
    mask = np.where(seen, 0.0, -1e30).transpose(1, 0, 2)
    mask = np.tile(mask, (1, 1, 4)).astype(ml_dtypes.bfloat16)

    arrays = {
        "xT": t("L0_attn_x").reshape(TOK, D).T, "cT": t("L0_c").T, "wmod": t("L0_wmod"),
        "w_inT": t("L0_attn_W_in").T, "w_x0": t("L0_attn_W_x")[0:1], "w_dt": t("L0_attn_W_dt").reshape(1, D),
        "b_dt": t("L0_attn_b_dt").reshape(D, 1), "gamma": t("L0_attn_gamma").reshape(D, 1),
        "beta": t("L0_attn_beta").reshape(D, 1),
        "wqkv": t("L0_ffn_wqkv"), "q_scale": t("L0_ffn_q_scale"), "k_scale": t("L0_ffn_k_scale"),
        "wo": t("L0_ffn_wo"), "ln_g": t("L0_ffn_ln_g"), "ln_b": t("L0_ffn_ln_b"), "w1": t("L0_ffn_w1"),
        "b1": t("L0_ffn_b1"), "w2": t("L0_ffn_w2"), "b2": t("L0_ffn_b2"),
        "rot_tab": rot_tab, "mask": mask, "ident_bf": np.eye(128, dtype=ml_dtypes.bfloat16),
        "ident": np.eye(128, dtype=np.float32),
    }
    nc = bacc.Bacc("TRN2", target_bir_lowering=False, num_devices=1)
    feeds, args = {}, {}
    for name, a in arrays.items():
        a = np.ascontiguousarray(a)
        feeds[f"in_{name}"] = a
        args[name] = nc.dram_tensor(f"in_{name}", a.shape, mybir.dt.from_np(a.dtype), kind="ExternalInput").ap()
    args["outT"] = nc.dram_tensor("outT", (D, TOK), F32, kind="ExternalOutput").ap()
    build(nc, **args)
    r = run_bass_kernel_spmd(nc, [feeds], core_ids=[0])
    return np.ascontiguousarray(r.results[0]["outT"].T).reshape(SEQS, L, D)
```

```python
from contextlib import ExitStack

import concourse.bass as bass
from concourse import mybir

ALU = mybir.AluOpType
ACT = mybir.ActivationFunctionType
F32 = mybir.dt.float32
F32R = mybir.dt.float32r
BF16 = mybir.dt.bfloat16
AX = mybir.AxisListType

D = 128
SEQS = 32
L = 256
TOK = SEQS * L
TILES = L // 128
DEPTH = 2
HEADS = 8
DH = 64
INNER = HEADS * DH
PAIRS = HEADS // 2
HID = 341
CHUNKS = [(0, 128), (128, 128), (256, HID - 256)]
WIN = 64
LN_EPS = 1e-5
STAGES = 5
STEP = 512
STEPS = TOK // STEP
LN2 = 0.6931471805599453
NORM_SHIFT = 20
W_LOADS = 3 + 3 * 3 + 2 + 3

ONCE = (
    "consts_in x_first x_rest w_in mod_in consts_set silu_sig silu_done mod_mm mod_gate outer_mm "
    "outer_set w_hi w_ready o_comp o_st"
).split()
STEPPED = {
    "tensor": (
        "b_mean0 b_mean1 b_mean2 b_var0 b_var1 b_var2 b_xz b_dtmm "
        "q_proj0 q_proj1 v_proj0 v_proj1 qT_mm0 qT_mm1 kT_mm0 kT_mm1 s_mm0 s_mm1 pT_mm00 pT_mm01 pT_mm10 "
        "pT_mm11 oT_mm0 oT_mm1 wo_mm c_mean c_var c_up0 c_up1 c_up2 c_down").split(),
    "scalar": (
        "b_sq0 b_sq1 b_sq2 b_ln0 b_ln1 b_ln2 b_rstd0 b_rstd1 b_rstd2 b_tanh b_gate b_dt b_decay "
        "qk_sq0 qk_sq1 v_sb1 qk_ln0 qk_ln1 qk_r0 qk_r1 kT0 s_exp0 s_exp1 pT00 pT11 oT0 oT1 c_ln c_rstd "
        "c_hi c_gelu0 c_gelu1 c_gelu2").split(),
    "vector": (
        "b_dev0 b_dev1 b_dev2 b_xn0 b_xn1 b_xn2 b_h b_xh b_w b_scan b_lng b_x1 b_hB "
        "h_hi h_lo v_sb0 v_mix qk_ss0 qk_ss1 qk_clip0 qk_clip1 qk_na0 qk_na1 qk_nb0 qk_nb1 qk_nc0 qk_nc1 "
        "qk_n0 qk_n1 qT0 qT1 kT1 s_max0 s_max1 s_rec0 s_rec1 pT01 pT10 x_attn c_shift c_dev c_sq c_na "
        "c_nb c_nc c_xn c_aff c_lo c_act0 c_act1 c_act2 x_ffn").split(),
    "gpsimd": (
        "b_g "
        "rot_u0 rot_u1 rot_w0 rot_w1 rot0 rot1 s_norm0 s_norm1").split(),
}


class Signals:

    def __init__(self, nc, ctx):
        names = ONCE + [n for group in STEPPED.values() for n in group]
        self.by_name = {n: ctx.enter_context(nc.semaphore(n)) for n in names}

    def __getitem__(self, name):
        return self.by_name[name]


class Stage:

    def __init__(self, on, n, col, item, par, layer):
        self.on, self.n, self.col, self.item, self.par, self.layer = on, n, col, item, par, layer
        self.done = n + 1 if on else n


def pipeline(eng, depth, items, rounds, unroll, width, step):

    def fixed(m):
        st = []
        for k in range(depth):
            q = m - k
            on = 0 <= q < items * rounds
            b = q % items
            st.append(Stage(on, min(max(q, 0), items * rounds) + 1, b * width, b, q % 2, q // items))
        step(*st)

    lead = depth - 1 + (items - depth + 1) % unroll
    for r in range(rounds):
        for m in range(lead):
            fixed(r * items + m)
        with eng.Fori(0, (items - lead) // unroll) as i:
            for s in range(unroll):
                st = []
                for k in range(depth):
                    b = eng.snap(i * unroll + (lead + s - k))
                    st.append(Stage(True, eng.snap(b + (r * items + 1)), eng.snap(b * width), b,
                                    (lead + s - k) % 2, r))
                step(*st)
    for m in range(depth - 1):
        fixed(rounds * items + m)


def build(nc, xT, cT, wmod, w_inT, w_x0, w_dt, b_dt, gamma, beta, wqkv, q_scale, k_scale, wo,
          ln_g, ln_b, w1, b1, w2, b2, rot_tab, mask, ident_bf, ident, outT):
    with ExitStack() as ctx:
        def sb(name, shape, dt=F32):
            return ctx.enter_context(nc.sbuf_tensor(name, shape, dt))

        sig = Signals(nc, ctx)
        ps = ctx.enter_context(nc.psum_tensor("ps", [128, 8, 512], F32))
        BANK = {
            "q_proj0": 4, "q_proj1": 4, "v_proj0": 6, "v_proj1": 7, "qT_mm0": 0, "qT_mm1": 2,
            "kT_mm0": 6, "kT_mm1": 6, "s_mm0": 0, "s_mm1": 0, "pT_mm00": 1, "pT_mm01": 6, "pT_mm10":
            2, "pT_mm11": 3, "oT_mm0": 6, "oT_mm1": 2, "wo_mm": 3, "c_mean": 3, "c_var": 2, "c_up0":
            7, "c_up1": 2, "c_up2": 2, "c_down": 7}
        BX, BZ = 6, 7

        X = sb("X", [128, TOK])
        X1 = sb("X1", [128, TOK])
        idf = sb("idf", [128, 128])
        idb = sb("idb", [128, 128], BF16)
        avg = sb("avg", [128, 128])
        maskb = sb("maskb", [128, TILES, 512], BF16)
        tab = sb("tab", [128, TILES, 4, DH])
        rot = sb("rot", [128, DEPTH, TILES, 4, DH])
        qks = sb("qks", [128, DEPTH, 2, DH])
        biases = sb("biases", [128, 2])
        cTs = sb("cTs", [128, SEQS])
        csig = sb("csig", [128, SEQS])
        csilu = sb("csilu", [128, SEQS])
        mod = sb("mod", [128, 6, SEQS])
        gsgn = sb("gsgn", [128, 2, SEQS])
        gabs = sb("gabs", [128, 2, SEQS])
        winT = sb("winT", [128, 2 * D])
        wx = sb("wx", [1, D])
        wdt = sb("wdt", [1, D])
        wouter = sb("wouter", [128, D])
        vec = sb("vec", [128, 3])
        wq_hi = [sb(f"wq_hi{l}", [128, 3 * INNER], F32R) for l in range(DEPTH)]
        wq_lo = [sb(f"wq_lo{l}", [128, 3 * INNER], F32R) for l in range(DEPTH)]
        w1_hi = [sb(f"w1_hi{l}", [128, 2 * HID], F32R) for l in range(DEPTH)]
        w1_lo = [sb(f"w1_lo{l}", [128, 2 * HID], F32R) for l in range(DEPTH)]
        wos = sb("wos", [128, DEPTH, PAIRS, D])
        w2s = sb("w2s", [128, DEPTH, 3, D])
        lvec = sb("lvec", [128, DEPTH, 3])
        b1s = sb("b1s", [128, DEPTH, 2, 3])
        h_hi = sb("h_hi_t", [128, L], F32R)
        h_lo = sb("h_lo_t", [128, L], F32R)
        qk_sq = sb("qk_sq", [128, 2 * INNER])
        ss = sb("ss", [128, TILES, 2 * HEADS])
        lnss = sb("lnss", [128, TILES, 2 * HEADS])
        rn = sb("rn", [128, TILES, 2 * HEADS])
        nwt = sb("nwt", [128, TILES, 2 * HEADS])
        qk_n = sb("qk_n", [128, TILES, 2 * INNER])
        qk_u = sb("qk_u", [128, TILES, 2 * INNER])
        qk_w = sb("qk_w", [128, 2 * INNER])
        V = sb("V", [128, 2, TILES + 1, INNER])
        qT = sb("qT_t", [128, PAIRS, L])
        kT = sb("kT_t", [128, PAIRS, L])
        nmax = sb("nmax", [128, TILES, HEADS])
        lsum = sb("lsum", [128, TILES, HEADS])
        lrec = sb("lrec", [128, TILES, HEADS])
        prob = sb("prob", [128, TILES, HEADS, 128])
        pT = sb("pT_t", [128, HEADS, 128])
        oT = sb("oT_t", [128, PAIRS, L])
        hs = sb("hs", [128, L])
        dev = sb("dev", [128, L])
        csq = sb("csq", [128, L])
        crstd = sb("crstd", [128, L])
        cnwt = sb("cnwt", [128, L])
        f_hi = sb("f_hi", [128, L], F32R)
        f_lo = sb("f_lo", [128, L], F32R)
        gel = sb("gel", [128, 3, L])
        act_ = sb("act_", [128, 3, L])
        cln, xn, hn = csq, cnwt, dev

        room = [t[:, c:c + 2, :].rearrange("p c k -> p (c k)") for t in (qT, kT, oT) for c in (0, 2)]
        room += [V[:, p, t, :] for p in range(2) for t in range(3)]
        room += [prob[:, t, h:h + 4, :].rearrange("p h k -> p (h k)") for t in range(2) for h in (0, 4)]
        B = dict(zip("d0 d1 d2 sq0 sq1 sq2 ln r0 r1 r2 xn h tanh dt gate decay".split(), room))
        B["w"] = pT[:, 0:4, :].rearrange("p h k -> p (h k)")
        B["y"] = pT[:, 4:8, :].rearrange("p h k -> p (h k)")
        B["g"] = gel[:, 0:2, :].rearrange("p h k -> p (h k)")
        B["ln1"] = act_[:, 0:2, :].rearrange("p h k -> p (h k)")
        wmods = X[:, 0:6 * D]
        flat = lambda t: t.rearrange("p t n -> p (t n)")
        wq_raw = [flat(qk_n[:])[:, 0:3 * INNER], flat(qk_u[:])[:, 0:3 * INNER]]
        w1_raw = [qk_w[:, 0:2 * HID], qk_sq[:, 0:2 * HID]]

        def heads(ap, n):
            return ap.rearrange("p (h d) -> p h d", h=n)

        def shifted(col):
            return ((slice(0, 64), bass.ds(col, L), slice(0, L)),
                    (slice(64, 128), bass.ds(col, L - 1), slice(1, L)))

        def raise_once(eng, names):
            for name in names:
                eng.sem_inc(sig[name], 1)

        def branch(eng, step):
            pipeline(eng, 6, STEPS, 1, 1, STEP, step)

        def layers(eng, step):
            pipeline(eng, STAGES, SEQS, DEPTH, 2, L, step)

        def two_before(eng, name, s):
            if not isinstance(s.n, int) or s.n > 2:
                eng.wait_ge(sig[name], s.n - 1)

        def full(name):
            return ps[:, BANK[name], :]

        def two(name):
            return ps[:, BANK[name]:BANK[name] + 2, :]

        def pairs(name):
            return ps[:, BANK[name], :].rearrange("p (c k) -> p c k", c=PAIRS)

        def half(name):
            return ps[:, BANK[name], 0:L]

        N_CONST = 12
        FIRST = 2 * STEP
        block = ctx.enter_context(nc.Block())

        @block.sync
        def _(sp):
            sp.dma_start(X1[:, 0:FIRST], xT[:, 0:FIRST]).then_inc(sig["x_first"], 16)
            for dst, src in ((cTs[:], cT), (wmods, wmod), (winT[:], w_inT),
                             (wx[:], w_x0), (wdt[:], w_dt), (vec[:, 0:1], b_dt),
                             (vec[:, 1:2], gamma), (vec[:, 2:3], beta),
                             (idf[:], ident), (idb[:], ident_bf), (maskb[:], mask), (tab[:], rot_tab)):
                sp.dma_start(dst, src).then_inc(sig["consts_in"], 16)
            sp.dma_start(X1[:, FIRST:], xT[:, FIRST:]).then_inc(sig["x_rest"], 16)
            for l in range(DEPTH):
                loads = [(wq_raw[l], wqkv[l]), (w1_raw[l], w1[l]),
                         (wos[:, l], wo[l].rearrange("(c p) n -> p c n", p=128)),
                         (qks[:, l, 0, :], q_scale[l:l + 1].broadcast_to([128, DH])),
                         (qks[:, l, 1, :], k_scale[l:l + 1].broadcast_to([128, DH]))]
                for c, (lo, n) in enumerate(CHUNKS):
                    loads.append((w2s[0:n, l, c, :], w2[l, lo:lo + n]))
                    for half in range(2):
                        o = half * HID + lo
                        loads.append((b1s[0:n, l, half, c:c + 1], b1[l:l + 1, o:o + n].rearrange("a p -> p a")))
                for c, v in enumerate((ln_g, ln_b, b2)):
                    loads.append((lvec[:, l, c:c + 1], v[l:l + 1].rearrange("a p -> p a")))
                assert len(loads) == W_LOADS
                for dst, src in loads:
                    sp.dma_start(dst, src).then_inc(sig["w_in"], 16)
            for b in range(0, SEQS, 4):
                sp.wait_ge(sig["o_comp"], b + 4)
                o = slice(b * L, (b + 4) * L)
                sp.dma_start(outT[:, o], X1[:, o]).then_inc(sig["o_st"], 16)
            sp.wait_ge(sig["o_st"], 16 * (SEQS // 4))

        @block.tensor
        def _(pe):
            mm = nc.tensor.matmul
            raise_once(pe, STEPPED["tensor"])
            pe.wait_ge(sig["silu_done"], 1)
            pe.wait_ge(sig["consts_in"], 16 * N_CONST)
            for j in range(6):
                last = mm(ps[:, BX, SEQS * j:SEQS * (j + 1)], wmods[:, D * j:D * (j + 1)], csilu[:],
                          start=True, stop=True)
            last.then_inc(sig["mod_mm"], 1)
            mm(ps[:, BZ, 0:D], wx[:], wdt[:], start=True, stop=True).then_inc(sig["outer_mm"], 1)
            pe.wait_ge(sig["outer_set"], 1)
            pe.wait_ge(sig["mod_gate"], 1)
            pe.wait_ge(sig["consts_set"], 1)
            pe.wait_ge(sig["x_first"], 16)

            def branch_step(A, Bs, C, Ds, E, F):
                def mean(k, st, src):
                    pe.wait_ge(sig[f"b_dev{k}"], st.n)
                    mm(ps[:, k, :], avg[:], src, start=True, stop=True).then_inc(sig[f"b_mean{k}"], 1)

                def var(k, st, nxt):
                    pe.wait_ge(sig[f"b_sq{k}"], st.n + 1)
                    pe.wait_ge(sig[f"b_ln{k}"], nxt.done)
                    mm(ps[:, 3 + k, :], avg[:], B[f"sq{k}"], start=True, stop=True).then_inc(sig[f"b_var{k}"], 1)

                if A.on:
                    if not isinstance(A.item, int) or A.item >= FIRST // STEP:
                        pe.wait_ge(sig["x_rest"], 16)
                    mean(0, A, X1[:, bass.ds(A.col, STEP)])
                if Ds.on:
                    pe.wait_ge(sig["b_g"], Ds.n + 1)
                    mean(1, Ds, B["g"])
                if C.on:
                    pe.wait_ge(sig["b_tanh"], C.n + 1)
                    mm(ps[:, BX, :], wouter[:], B["tanh"], start=True, stop=True).then_inc(sig["b_dtmm"], 1)
                if E.on:
                    pe.wait_ge(sig["b_x1"], E.n + 1)
                    mean(2, E, X1[:, bass.ds(E.col, STEP)])
                if Ds.on: var(1, Ds, E)
                if Bs.on:
                    pe.wait_ge(sig["b_h"], Bs.n + 1)
                    pe.wait_ge(sig["b_dt"], C.done)
                    pe.wait_ge(sig["b_gate"], C.done)
                    mm(ps[:, BX, :], winT[:, 0:D], B["h"], start=True, stop=True)
                    mm(ps[:, BZ, :], winT[:, D:2 * D], B["h"], start=True, stop=True).then_inc(sig["b_xz"], 1)
                if A.on: var(0, A, Bs)
                if E.on: var(2, E, F)

            branch(pe, branch_step)
            pe.wait_ge(sig["w_ready"], DEPTH)
            pe.wait_ge(sig["w_in"], 16 * W_LOADS * DEPTH)
            pe.wait_ge(sig["b_dt"], STEPS + 1)
            pe.wait_ge(sig["b_ln2"], STEPS + 1)
            pe.wait_ge(sig["b_dev2"], STEPS + 1)

            def step(*st):
                def q_k_project(s, t):
                    if t == 0:
                        pe.wait_ge(sig["h_hi"], s.n + 1)
                        pe.wait_ge(sig["h_lo"], s.n + 1)
                    tok = slice(128 * t, 128 * t + 128)
                    hi, lo = wq_hi[s.layer], wq_lo[s.layer]
                    for j in range(2):
                        o, dst = slice(INNER * j, INNER * j + INNER), ps[:, BANK[f"q_proj{t}"] + j, :]
                        mm(dst, h_hi[:, tok], lo[:, o], start=True, stop=False)
                        mm(dst, h_lo[:, tok], hi[:, o], start=False, stop=False)
                        last = mm(dst, h_hi[:, tok], hi[:, o], start=False, stop=True)
                    last.then_inc(sig[f"q_proj{t}"], 1)

                def v_project(s, t):
                    tok, o = slice(128 * t, 128 * t + 128), slice(2 * INNER, 3 * INNER)
                    hi, lo, dst = wq_hi[s.layer], wq_lo[s.layer], ps[:, BANK[f"v_proj{t}"], :]
                    mm(dst, h_hi[:, tok], lo[:, o], start=True, stop=False)
                    mm(dst, h_lo[:, tok], hi[:, o], start=False, stop=False)
                    mm(dst, h_hi[:, tok], hi[:, o], start=False, stop=True).then_inc(sig[f"v_proj{t}"], 1)

                def q_transpose(s, t):
                    pe.wait_ge(sig[f"rot{t}"], s.n + 1)
                    for c in range(PAIRS):
                        o = 128 * c
                        last = nc.tensor.transpose(ps[:, BANK[f"qT_mm{t}"], 128 * c:128 * c + 128], qk_u[:, t, o:o + 128], idf[:])
                    last.then_inc(sig[f"qT_mm{t}"], 1)

                def k_transpose(s, t):
                    pe.wait_ge(sig[f"rot{t}"], s.n + 1)
                    for c in range(PAIRS):
                        o = INNER + 128 * c
                        last = nc.tensor.transpose(ps[:, BANK[f"kT_mm{t}"], 128 * c:128 * c + 128], qk_u[:, t, o:o + 128], idf[:])
                    last.then_inc(sig[f"kT_mm{t}"], 1)

                def scores(s, t):
                    pe.wait_ge(sig[f"qT{t}"], s.n + 1)
                    pe.wait_ge(sig[f"kT{t}"], s.n + 1)
                    if t == 1:
                        pe.wait_ge(sig["kT0"], s.n + 1)
                    bank = BANK[f"s_mm{t}"]
                    for r in range(2):
                        mm(ps[:, bank + r, :], idb[:], maskb[:, t, :], start=True, stop=True)
                    for c in range(PAIRS):
                        o = slice(128 * c, 128 * c + 128)
                        if t == 0:
                            for r in range(2):
                                rows = slice(64 * r, 64 * r + 64)
                                last = mm(ps[:, bank + r, o], qT[rows, c, 0:128], kT[rows, c, 0:128],
                                          start=False, stop=True, skip_group_check=True)
                        else:
                            for w, r in ((2, 0), (3, 1), (2, 1), (3, 0)):
                                rows = slice(64 * r, 64 * r + 64)
                                if w == 2:
                                    dst = ps[0:64, bank + r, o].rearrange("p (w k) -> p w k", w=2)
                                    keys = kT[rows, c, 64:192].rearrange("p (w k) -> p w k", w=2)[:, ::-1, :]
                                else:
                                    dst, keys = ps[64:128, bank + r, o], kT[rows, c, 128:256]
                                last = mm(dst, qT[rows, c, 64 * w:64 * w + 64], keys,
                                          start=False, stop=True, skip_group_check=True)
                    last.then_inc(sig[f"s_mm{t}"], 1)

                def prob_transpose(s, t, half):
                    pe.wait_ge(sig[f"s_norm{t}"], s.n + 1)
                    for j in range(4):
                        c, r = 2 * half + j // 2, j % 2
                        last = nc.tensor.transpose(ps[:, BANK[f"pT_mm{t}{half}"], 128 * j:128 * j + 128],
                                                   prob[:, t, 4 * r + c, :], idf[:])
                    last.then_inc(sig[f"pT_mm{t}{half}"], 1)

                def attend(s, t):
                    pe.wait_ge(sig["v_mix" if t else "v_sb0"], s.n + 1)
                    bank = BANK[f"oT_mm{t}"]
                    for half in range(2):
                        pe.wait_ge(sig[f"pT{t}{half}"], s.n + 1)
                        for j in range(4):
                            c, r = 2 * half + j // 2, j % 2
                            rows = slice(64 * r, 64 * r + 64)
                            feat = slice(DH * (2 * c + r), DH * (2 * c + r) + DH)
                            if t == 0:
                                last = mm(ps[rows, bank, 128 * c:128 * c + 128], V[:, s.par, 0, feat],
                                          pT[:, 2 * c + r, :], start=True, stop=True)
                            else:
                                mm(ps[rows, bank, 128 * c:128 * c + 64], V[:, s.par, TILES, feat],
                                   pT[:, 2 * c + r, 0:64], start=True, stop=True)
                                last = mm(ps[rows, bank, 128 * c + 64:128 * c + 128], V[:, s.par, 1, feat],
                                          pT[:, 2 * c + r, 64:128], start=True, stop=True)
                    last.then_inc(sig[f"oT_mm{t}"], 1)

                def out_proj(s):
                    pe.wait_ge(sig["oT0"], s.n + 1)
                    pe.wait_ge(sig["oT1"], s.n + 1)
                    for c in range(PAIRS):
                        last = mm(half("wo_mm"), wos[:, s.layer, c, :], oT[:, c, :], start=(c == 0), stop=(c == PAIRS - 1))
                    last.then_inc(sig["wo_mm"], 1)

                def c_mean(s):
                    pe.wait_ge(sig["c_shift"], s.n + 1)
                    mm(half("c_mean"), avg[:], hs[:], start=True, stop=True).then_inc(sig["c_mean"], 1)

                def c_var(s):
                    pe.wait_ge(sig["c_sq"], s.n + 1)
                    mm(half("c_var"), avg[:], csq[:], start=True, stop=True).then_inc(sig["c_var"], 1)

                def c_up(s, k):
                    pe.wait_ge(sig["c_lo"], s.n + 1)
                    lo, m = CHUNKS[k]
                    hi_w, lo_w = w1_hi[s.layer], w1_lo[s.layer]
                    for value in range(2):
                        o = slice((1 - value) * HID + lo, (1 - value) * HID + lo + m)
                        dst = ps[0:m, BANK[f"c_up{k}"], value * L:value * L + L]
                        mm(dst, lo_w[:, o], f_hi[:], start=True, stop=False)
                        mm(dst, hi_w[:, o], f_lo[:], start=False, stop=False)
                        last = mm(dst, hi_w[:, o], f_hi[:], start=False, stop=True)
                    last.then_inc(sig[f"c_up{k}"], 1)

                def c_down(s):
                    for k, (lo, m) in enumerate(CHUNKS):
                        pe.wait_ge(sig[f"c_act{k}"], s.n + 1)
                        last = mm(half("c_down"), w2s[0:m, s.layer, k, :], act_[0:m, k, :], start=(k == 0), stop=(k == 2))
                    last.then_inc(sig["c_down"], 1)

                if st[3].on:
                    pe.wait_ge(sig["pT11"], st[2].n)
                    if not st[2].on:
                        pe.wait_ge(sig["c_dev"], st[3].n)
                        pe.wait_ge(sig["x_attn"], st[3].n)
                    out_proj(st[3])
                if st[4].on:
                    pe.wait_ge(sig["oT1"], st[2].n)
                    if not st[2].on:
                        pe.wait_ge(sig["pT10"], st[2].n)
                        pe.wait_ge(sig["qT1"], st[1].n)
                        pe.wait_ge(sig["c_na"], st[3].n)
                        pe.wait_ge(sig["c_act2"], st[4].n)
                        pe.wait_ge(sig["c_act1"], st[4].n)
                    c_up(st[4], 1)
                if st[1].on:
                    pe.wait_ge(sig["v_sb0"], st[0].n)
                    if not st[0].on:
                        pe.wait_ge(sig["kT1"], st[1].n)
                        pe.wait_ge(sig["oT0"], st[2].n)
                        pe.wait_ge(sig["pT01"], st[2].n)
                        pe.wait_ge(sig["kT0"], st[1].n)
                    k_transpose(st[1], 0)
                if st[1].on:
                    pe.wait_ge(sig["s_exp1"], st[1].n)
                    q_transpose(st[1], 0)
                if st[0].on:
                    pe.wait_ge(sig["qk_n1"], st[0].n)
                    q_k_project(st[0], 0)
                if st[2].on:
                    pe.wait_ge(sig["s_exp1"], st[1].n)
                    if not st[1].on:
                        pe.wait_ge(sig["s_exp0"], st[1].n)
                        pe.wait_ge(sig["pT00"], st[2].n)
                    prob_transpose(st[2], 0, 0)
                if st[3].on:
                    pe.wait_ge(sig["x_attn"], st[3].done)
                    c_mean(st[3])
                if st[4].on:
                    pe.wait_ge(sig["v_sb1"], st[0].n)
                    if not st[0].on:
                        pe.wait_ge(sig["x_ffn"], st[4].n)
                        pe.wait_ge(sig["c_act0"], st[4].n)
                    c_up(st[4], 0)
                if st[4].on:
                    pe.wait_ge(sig["c_act1"], st[4].done)
                    c_up(st[4], 2)
                if st[2].on:
                    pe.wait_ge(sig["kT0"], st[1].done)
                    if not st[1].on:
                        pe.wait_ge(sig["v_sb0"], st[0].n)
                        pe.wait_ge(sig["kT1"], st[1].n)
                        pe.wait_ge(sig["oT0"], st[2].n)
                        pe.wait_ge(sig["pT01"], st[2].n)
                    prob_transpose(st[2], 0, 1)
                if st[1].on:
                    pe.wait_ge(sig["pT00"], st[2].done)
                    pe.wait_ge(sig["qT0"], st[1].done)
                    if not st[2].on:
                        pe.wait_ge(sig["s_exp1"], st[1].n)
                        pe.wait_ge(sig["s_exp0"], st[1].n)
                    scores(st[1], 0)
                if st[3].on:
                    pe.wait_ge(sig["c_act2"], st[4].done)
                    if not st[4].on:
                        pe.wait_ge(sig["c_act1"], st[4].done)
                        pe.wait_ge(sig["oT1"], st[2].n)
                        pe.wait_ge(sig["pT10"], st[2].n)
                        pe.wait_ge(sig["qT1"], st[1].n)
                        pe.wait_ge(sig["c_na"], st[3].n)
                    c_var(st[3])
                if st[2].on:
                    pe.wait_ge(sig["pT01"], st[2].done)
                    attend(st[2], 0)
                if st[4].on:
                    pe.wait_ge(sig["c_act0"], st[4].done)
                    c_down(st[4])
                if st[2].on:
                    pe.wait_ge(sig["c_dev"], st[3].done)
                    if not st[3].on:
                        pe.wait_ge(sig["x_attn"], st[3].done)
                        pe.wait_ge(sig["pT11"], st[2].n)
                    prob_transpose(st[2], 1, 1)
                if st[1].on:
                    pe.wait_ge(sig["c_na"], st[3].done)
                    if not st[3].on:
                        pe.wait_ge(sig["c_act2"], st[4].done)
                        pe.wait_ge(sig["c_act1"], st[4].done)
                        pe.wait_ge(sig["oT1"], st[2].n)
                        pe.wait_ge(sig["pT10"], st[2].n)
                        pe.wait_ge(sig["qT1"], st[1].n)
                    q_transpose(st[1], 1)
                if st[1].on:
                    pe.wait_ge(sig["oT0"], st[2].done)
                    if not st[2].on:
                        pe.wait_ge(sig["pT01"], st[2].done)
                        pe.wait_ge(sig["kT0"], st[1].done)
                        pe.wait_ge(sig["v_sb0"], st[0].n)
                        pe.wait_ge(sig["kT1"], st[1].n)
                    k_transpose(st[1], 1)
                if st[0].on:
                    pe.wait_ge(sig["qk_n0"], st[0].done)
                    q_k_project(st[0], 1)
                if st[2].on:
                    pe.wait_ge(sig["qT1"], st[1].done)
                    if not st[1].on:
                        pe.wait_ge(sig["c_na"], st[3].done)
                        pe.wait_ge(sig["c_act2"], st[4].done)
                        pe.wait_ge(sig["c_act1"], st[4].done)
                        pe.wait_ge(sig["oT1"], st[2].n)
                        pe.wait_ge(sig["pT10"], st[2].n)
                    prob_transpose(st[2], 1, 0)
                if st[1].on:
                    pe.wait_ge(sig["s_exp0"], st[1].done)
                    scores(st[1], 1)
                if st[2].on:
                    pe.wait_ge(sig["pT10"], st[2].done)
                    attend(st[2], 1)
                if st[0].on:
                    pe.wait_ge(sig["kT1"], st[1].done)
                    if not st[1].on:
                        pe.wait_ge(sig["oT0"], st[2].done)
                        pe.wait_ge(sig["pT01"], st[2].done)
                        pe.wait_ge(sig["kT0"], st[1].done)
                        pe.wait_ge(sig["v_sb0"], st[0].n)
                    v_project(st[0], 0)
                if st[0].on:
                    pe.wait_ge(sig["x_ffn"], st[4].done)
                    if not st[4].on:
                        pe.wait_ge(sig["c_act0"], st[4].done)
                        pe.wait_ge(sig["v_sb1"], st[0].n)
                    v_project(st[0], 1)
            layers(pe, step)

        @block.scalar
        def _(act):
            f = nc.scalar.activation
            raise_once(act, STEPPED["scalar"])
            act.wait_ge(sig["consts_in"], 16 * N_CONST)
            f(csig[:], cTs[:], ACT.Sigmoid).then_inc(sig["silu_sig"], 1)
            act.wait_ge(sig["consts_set"], 1)

            def branch_step(A, Bs, C, Ds, E, F):
                def square(k, st):
                    act.wait_ge(sig[f"b_dev{k}"], st.n + 1)
                    act.wait_ge(sig[f"b_var{k}"], st.n)
                    f(B[f"sq{k}"], B[f"d{k}"], ACT.Square).then_inc(sig[f"b_sq{k}"], 1)

                norms = [(2, F), (1, E), (0, Bs)]
                act.preload_act_table_set("natural_log")
                for k, st in norms:
                    if st.on:
                        act.wait_ge(sig[f"b_var{k}"], st.n + 1)
                        act.wait_ge(sig[f"b_xn{k}"], st.n)
                        f(B[f"r{k}"], ps[:, 3 + k, :], ACT.Ln, bias=biases[:, 0:1]).then_inc(sig[f"b_ln{k}"], 1)
                act.preload_act_table_set("exp_and_others")
                for k, st in norms:
                    if st.on:
                        act.wait_ge(sig[f"b_ln{k}"], st.n + 1)
                        f(B[f"r{k}"], B[f"r{k}"], ACT.Exp, scale=-0.5).then_inc(sig[f"b_rstd{k}"], 1)
                if C.on:
                    act.wait_ge(sig["b_xz"], C.n + 1)
                    act.wait_ge(sig["b_w"], C.n)
                    f(B["tanh"], ps[:, BX, :], ACT.Tanh).then_inc(sig["b_tanh"], 1)
                    act.preload_act_table_set("sigmoid_and_others")
                    act.wait_ge(sig["b_g"], Ds.done)
                    f(B["gate"], ps[:, BZ, :], ACT.Sigmoid).then_inc(sig["b_gate"], 1)
                    act.wait_ge(sig["b_dtmm"], C.n + 1)
                    f(B["dt"], ps[:, BX, :], ACT.Sigmoid, bias=vec[:, 0:1]).then_inc(sig["b_dt"], 1)
                if Ds.on: square(1, Ds)
                if C.on:
                    act.wait_ge(sig["b_dt"], C.n + 1)
                    act.wait_ge(sig["b_scan"], Ds.done)
                    f(B["decay"], B["dt"], ACT.Sigmoid, scale=-1.0).then_inc(sig["b_decay"], 1)
                if A.on: square(0, A)
                if E.on: square(2, E)

            branch(act, branch_step)
            act.wait_ge(sig["w_in"], 16 * W_LOADS * DEPTH)
            act.wait_ge(sig["w_ready"], DEPTH)
            act.wait_ge(sig["b_hB"], STEPS + 1)
            act.wait_ge(sig["b_var2"], STEPS + 1)

            def step(*st):
                def squares(s, t):
                    act.wait_ge(sig[f"q_proj{t}"], s.n + 1)
                    act.wait_ge(sig["qk_ss0"] if t else sig["qk_ss1"], s.n + t)
                    f(heads(qk_sq[:], 2), two(f"q_proj{t}"), ACT.Square).then_inc(sig[f"qk_sq{t}"], 1)

                def values(s, t):
                    act.wait_ge(sig[f"v_proj{t}"], s.n + 1)
                    two_before(act, f"oT_mm{t}", s)
                    two_before(act, "v_mix", s)
                    f(V[:, s.par, t, :], full(f"v_proj{t}"), ACT.Copy).then_inc(sig[f"v_sb{t}"], 1)

                def norm_ln(s, t):
                    act.wait_ge(sig[f"qk_clip{t}"], s.n + 1)
                    act.wait_ge(sig[f"qk_r{t}"], s.n)
                    f(lnss[:, t, :], ss[:, t, :], ACT.Ln, scale=float(2 ** NORM_SHIFT)).then_inc(sig[f"qk_ln{t}"], 1)

                def norm_exp(s, t):
                    act.wait_ge(sig[f"qk_ln{t}"], s.n + 1)
                    act.wait_ge(sig[f"qk_n{t}"], s.n)
                    f(rn[:, t, :], lnss[:, t, :], ACT.Exp, scale=-0.5, bias=biases[:, 1:2]).then_inc(sig[f"qk_r{t}"], 1)

                def k_transposed(s, t):
                    act.wait_ge(sig[f"kT_mm{t}"], s.n + 1)
                    act.wait_ge(sig["s_mm0"], s.n)
                    act.wait_ge(sig["s_mm1"], s.n)
                    f(kT[:, :, 128 * t:128 * t + 128], pairs(f"kT_mm{t}"), ACT.Copy).then_inc(sig[f"kT{t}"], 1)

                def exps(s, t):
                    act.wait_ge(sig[f"s_max{t}"], s.n + 1)
                    act.wait_ge(sig["pT_mm10"] if t else sig["pT_mm01"], s.n)
                    act.wait_ge(sig[f"s_rec{t}"], s.n)
                    for h in range(HEADS):
                        o = slice(128 * (h % 4), 128 * (h % 4) + 128)
                        last = f(prob[:, t, h, :], ps[:, BANK[f"s_mm{t}"] + h // 4, o], ACT.Exp,
                                 bias=nmax[:, t, h:h + 1], accum_out=lsum[:, t, h:h + 1])
                    last.then_inc(sig[f"s_exp{t}"], 1)

                def prob_copy(s, t, half):
                    act.wait_ge(sig[f"pT_mm{t}{half}"], s.n + 1)
                    act.wait_ge(sig["oT_mm0"] if t else sig["oT_mm1"], s.n + t)
                    f(pT[:, 4 * half:4 * half + 4, :], pairs(f"pT_mm{t}{half}"), ACT.Copy).then_inc(sig[f"pT{t}{half}"], 1)

                def attended(s, t):
                    act.wait_ge(sig[f"oT_mm{t}"], s.n + 1)
                    act.wait_ge(sig["wo_mm"], s.n)
                    f(oT[:, :, 128 * t:128 * t + 128], pairs(f"oT_mm{t}"), ACT.Copy).then_inc(sig[f"oT{t}"], 1)

                def c_logarithm(s):
                    act.wait_ge(sig["c_var"], s.n + 1)
                    f(cln[:], half("c_var"), ACT.Ln, bias=biases[:, 0:1]).then_inc(sig["c_ln"], 1)

                def c_root(s):
                    act.wait_ge(sig["c_ln"], s.n + 1)
                    act.wait_ge(sig["c_nc"], s.n)
                    f(crstd[:], cln[:], ACT.Exp, scale=-0.5).then_inc(sig["c_rstd"], 1)

                def c_high(s):
                    act.wait_ge(sig["c_aff"], s.n + 1)
                    act.wait_ge(sig["c_up2"], s.n)
                    act.wait_ge(sig["c_lo"], s.n)
                    f(f_hi[:], hn[:], ACT.Copy).then_inc(sig["c_hi"], 1)

                def gelu(s, k):
                    m = CHUNKS[k][1]
                    act.wait_ge(sig[f"c_up{k}"], s.n + 1)
                    act.wait_ge(sig[f"c_act{k}"], s.n)
                    f(gel[0:m, k, :], ps[0:m, BANK[f"c_up{k}"], 0:L], ACT.Gelu,
                      bias=b1s[0:m, s.layer, 1, k:k + 1]).then_inc(sig[f"c_gelu{k}"], 1)

                if st[1].on: values(st[1], 1)
                if st[4].on: gelu(st[4], 1)
                if st[1].on: k_transposed(st[1], 0)
                if st[0].on: squares(st[0], 0)
                if st[2].on: prob_copy(st[2], 0, 0)
                if st[4].on: gelu(st[4], 0)
                if st[4].on: gelu(st[4], 2)
                act.preload_act_table_set("natural_log_exp_and_others")
                if st[0].on: norm_ln(st[0], 0)
                if st[0].on: norm_exp(st[0], 0)
                if st[3].on: c_logarithm(st[3])
                if st[3].on: c_root(st[3])
                if st[2].on: attended(st[2], 0)
                if st[1].on: exps(st[1], 0)
                if st[2].on: prob_copy(st[2], 1, 1)
                if st[0].on: squares(st[0], 1)
                if st[0].on: norm_ln(st[0], 1)
                if st[0].on: norm_exp(st[0], 1)
                if st[3].on: c_high(st[3])
                if st[2].on: attended(st[2], 1)
                if st[1].on: exps(st[1], 1)
                act.preload_act_table_set("gelu_and_others")
            layers(act, step)

        @block.vector
        def _(dve):
            v = nc.vector
            raise_once(dve, STEPPED["vector"])
            v.memset(avg[:], 1.0 / D)
            v.memset(biases[:, 0:1], LN_EPS)
            v.memset(biases[:, 1:2], NORM_SHIFT / 2 * LN2)
            v.memset(h_hi[64:128, 0:1].bitcast(F32), 0.0)
            v.memset(h_lo[64:128, 0:1].bitcast(F32), 0.0)
            v.memset(hs[64:128, 0:1], 0.0).then_inc(sig["consts_set"], 1)
            dve.wait_ge(sig["silu_sig"], 1)
            v.tensor_tensor(csilu[:], cTs[:], csig[:], ALU.mult).then_inc(sig["silu_done"], 1)
            dve.wait_ge(sig["mod_mm"], 1)
            modp = ps[:, BX, 0:6 * SEQS].rearrange("p (j b) -> p j b", j=6)
            for j in range(6):
                v.tensor_scalar(mod[:, j, :], modp[:, j, :], 1.0 if j in (1, 4) else 0.0, None, ALU.add)
            dve.wait_ge(sig["outer_mm"], 1)
            v.tensor_copy(wouter[:], ps[:, BZ, 0:D]).then_inc(sig["outer_set"], 1)
            for s, j in enumerate((2, 5)):
                last = v.tensor_scalar(gsgn[:, s, :], modp[:, j, :], 0.0, 2.0, ALU.is_ge, ALU.mult)
            last.then_inc(sig["mod_in"], 1)
            dve.wait_ge(sig["mod_in"], 1)
            for s, j in enumerate((2, 5)):
                last = v.scalar_tensor_tensor(gabs[:, s, :], modp[:, j, :], -1.0, mod[:, j, :], ALU.mult, ALU.max)
            last.then_inc(sig["mod_in"], 1)
            dve.wait_ge(sig["mod_in"], 2)
            v.tensor_scalar(gabs[:], gabs[:], 0.25, None, ALU.max).then_inc(sig["mod_in"], 1)
            dve.wait_ge(sig["mod_in"], 3)
            for s, j in enumerate((2, 5)):
                last = v.scalar_tensor_tensor(mod[:, j, :], gsgn[:, s, :], -1.0, gabs[:, s, :], ALU.add, ALU.mult)
            last.then_inc(sig["mod_gate"], 1)
            dve.wait_ge(sig["mod_gate"], 1)

            def branch_step(A, Bs, C, Ds, E, F):
                def halves(st):
                    for b in range(2):
                        yield slice(L * b, L * b + L), bass.ds(st.col + L * b, L), bass.ds(st.item * 2 + b, 1)

                def deviation(k, st, nxt, src):
                    dve.wait_ge(sig[f"b_mean{k}"], st.n + 1)
                    dve.wait_ge(sig[f"b_xn{k}"], nxt.done)
                    v.tensor_tensor(B[f"d{k}"], src, ps[:, k, :], ALU.subtract).then_inc(sig[f"b_dev{k}"], 1)

                def normalised(k, st, last_use):
                    dve.wait_ge(sig[f"b_rstd{k}"], st.n + 1)
                    for name, count in last_use:
                        dve.wait_ge(sig[name], count)
                    v.tensor_tensor(B["xn"], B[f"d{k}"], B[f"r{k}"], ALU.mult).then_inc(sig[f"b_xn{k}"], 1)
                    dve.wait_ge(sig[f"b_xn{k}"], st.n + 1)

                if Ds.on:
                    dve.wait_ge(sig["b_w"], Ds.n + 1)
                    dve.wait_ge(sig["b_decay"], Ds.n + 1)
                    dve.wait_ge(sig["b_g"], Ds.n)
                    for o, _, _ in halves(Ds):
                        last = v.tensor_tensor_scan(B["y"][:, o], B["decay"][:, o], B["w"][:, o], 0.0,
                                                    ALU.mult, ALU.subtract)
                    last.then_inc(sig["b_scan"], 1)
                if F.on:
                    normalised(2, F, [("b_h", Bs.n)])
                    for o, cols, b in halves(F):
                        last = v.tensor_scalar(X[:, cols], B["xn"][:, o], mod[:, 4, b], mod[:, 3, b], ALU.mult, ALU.add)
                    last.then_inc(sig["b_hB"], 1)
                if E.on:
                    normalised(1, E, [("b_hB", F.done), ("b_h", Bs.n)])
                    dve.wait_ge(sig["b_x1"], E.n)
                    v.tensor_scalar(B["ln1"], B["xn"], vec[:, 1:2], vec[:, 2:3], ALU.mult, ALU.add).then_inc(sig["b_lng"], 1)
                    dve.wait_ge(sig["b_lng"], E.n + 1)
                    dve.wait_ge(sig["b_xh"], E.n + 1)
                    for o, cols, b in halves(E):
                        last = v.scalar_tensor_tensor(X1[:, cols], B["ln1"][:, o], mod[:, 2, b], X1[:, cols],
                                                      ALU.mult, ALU.add)
                    last.then_inc(sig["b_x1"], 1)
                if Ds.on:
                    dve.wait_ge(sig["b_g"], Ds.n + 1)
                    deviation(1, Ds, E, B["g"])
                if Bs.on:
                    normalised(0, Bs, [("b_lng", E.done), ("b_hB", F.done)])
                    dve.wait_ge(sig["b_xz"], Bs.n)
                    dve.wait_ge(sig["b_xh"], Bs.n)
                    for o, _, b in halves(Bs):
                        last = v.tensor_scalar(B["h"][:, o], B["xn"][:, o], mod[:, 1, b], mod[:, 0, b], ALU.mult, ALU.add)
                    last.then_inc(sig["b_h"], 1)
                    dve.wait_ge(sig["b_h"], Bs.n + 1)
                    dve.wait_ge(sig["b_dev0"], Bs.n + 1)
                    for o, cols, b in halves(Bs):
                        last = v.scalar_tensor_tensor(X1[:, cols], B["h"][:, o], mod[:, 2, b], X1[:, cols],
                                                      ALU.mult, ALU.add)
                    last.then_inc(sig["b_xh"], 1)
                if A.on:
                    deviation(0, A, Bs, X1[:, bass.ds(A.col, STEP)])
                if E.on:
                    dve.wait_ge(sig["b_x1"], E.n + 1)
                    deviation(2, E, F, X1[:, bass.ds(E.col, STEP)])
                if C.on:
                    dve.wait_ge(sig["b_decay"], C.n + 1)
                    dve.wait_ge(sig["b_scan"], Ds.done)
                    v.scalar_tensor_tensor(B["w"], B["decay"], -1.0, B["tanh"], ALU.add, ALU.mult).then_inc(sig["b_w"], 1)

            branch(dve, branch_step)
            dve.wait_ge(sig["b_hB"], STEPS + 1)
            dve.wait_ge(sig["w_ready"], DEPTH)
            dve.wait_ge(sig["b_var2"], STEPS + 1)

            def step(*st):
                def h_high(s):
                    if s.layer:
                        dve.wait_ge(sig["x_ffn"], s.n - SEQS + 1)
                    dve.wait_ge(sig["v_proj1"], s.n)
                    dve.wait_ge(sig["h_lo"], s.n)
                    for rows, src, dst in shifted(s.col):
                        last = v.tensor_scalar(h_hi[rows, dst], X[rows, src], 1.0, None, ALU.mult)
                    last.then_inc(sig["h_hi"], 1)

                def h_low(s):
                    dve.wait_ge(sig["h_hi"], s.n + 1)
                    dve.wait_ge(sig["v_proj1"], s.n)
                    for rows, src, dst in shifted(s.col):
                        last = v.tensor_tensor(h_lo[rows, dst], X[rows, src], h_hi[rows, dst].bitcast(F32), ALU.subtract)
                    last.then_inc(sig["h_lo"], 1)

                def values(s, t):
                    dve.wait_ge(sig[f"v_proj{t}"], s.n + 1)
                    two_before(dve, f"oT_mm{t}", s)
                    two_before(dve, "v_mix", s)
                    v.tensor_copy(V[:, s.par, t, :], full(f"v_proj{t}")).then_inc(sig[f"v_sb{t}"], 1)

                def mixed(s):
                    dve.wait_ge(sig["v_sb0"], s.n + 1)
                    dve.wait_ge(sig["v_sb1"], s.n + 1)
                    two_before(dve, "oT_mm1", s)
                    v.tensor_copy(V[0:64, s.par, TILES, :], V[0:64, s.par, 1, :])
                    v.tensor_copy(V[64:128, s.par, TILES, :], V[64:128, s.par, 0, :]).then_inc(sig["v_mix"], 1)

                def square_sums(s, t):
                    dve.wait_ge(sig[f"qk_sq{t}"], s.n + 1)
                    dve.wait_ge(sig[f"qk_na{t}"], s.n)
                    dve.wait_ge(sig[f"qk_ln{t}"], s.n)
                    v.tensor_reduce(ss[:, t, :], heads(qk_sq[:], 2 * HEADS), AX.X, ALU.add).then_inc(sig[f"qk_ss{t}"], 1)

                def clip(s, t):
                    dve.wait_ge(sig[f"qk_ss{t}"], s.n + 1)
                    v.tensor_scalar(ss[:, t, :], ss[:, t, :], 1e-24, None, ALU.max).then_inc(sig[f"qk_clip{t}"], 1)

                def newton_a(s, t):
                    dve.wait_ge(sig[f"qk_r{t}"], s.n + 1)
                    dve.wait_ge(sig[f"qk_nc{t}"], s.n)
                    v.tensor_tensor(nwt[:, t, :], ss[:, t, :], rn[:, t, :], ALU.mult).then_inc(sig[f"qk_na{t}"], 1)

                def newton_b(s, t):
                    dve.wait_ge(sig[f"qk_na{t}"], s.n + 1)
                    v.scalar_tensor_tensor(nwt[:, t, :], nwt[:, t, :], -0.5, rn[:, t, :], ALU.mult, ALU.mult)\
                        .then_inc(sig[f"qk_nb{t}"], 1)

                def newton_c(s, t):
                    dve.wait_ge(sig[f"qk_nb{t}"], s.n + 1)
                    v.scalar_tensor_tensor(rn[:, t, :], nwt[:, t, :], 1.5, rn[:, t, :], ALU.add, ALU.mult)\
                        .then_inc(sig[f"qk_nc{t}"], 1)

                def normed(s, t):
                    dve.wait_ge(sig[f"qk_nc{t}"], s.n + 1)
                    dve.wait_ge(sig[f"rot_u{t}"], s.n)
                    dve.wait_ge(sig[f"rot_w{t}"], s.n)
                    v.tensor_tensor(heads(qk_n[:, t, :], 2 * HEADS), two(f"q_proj{t}").rearrange("p b (h d) -> p (b h) d", h=HEADS),
                                    rn[:, t, :].unsqueeze(2).broadcast_to([128, 2 * HEADS, DH]),
                                    ALU.mult).then_inc(sig[f"qk_n{t}"], 1)

                def q_transposed(s, t):
                    dve.wait_ge(sig[f"qT_mm{t}"], s.n + 1)
                    dve.wait_ge(sig[f"s_mm{t}"], s.n)
                    v.tensor_copy(qT[:, :, 128 * t:128 * t + 128], pairs(f"qT_mm{t}")).then_inc(sig[f"qT{t}"], 1)

                def k_transposed(s, t):
                    dve.wait_ge(sig[f"kT_mm{t}"], s.n + 1)
                    dve.wait_ge(sig["s_mm0"], s.n)
                    dve.wait_ge(sig["s_mm1"], s.n)
                    v.tensor_copy(kT[:, :, 128 * t:128 * t + 128], pairs(f"kT_mm{t}")).then_inc(sig[f"kT{t}"], 1)

                def maxes(s, t):
                    dve.wait_ge(sig[f"s_mm{t}"], s.n + 1)
                    dve.wait_ge(sig[f"s_exp{t}"], s.n)
                    v.tensor_reduce(nmax[:, t, :], two(f"s_mm{t}").rearrange("p b (c k) -> p (b c) k", c=4),
                                    AX.X, ALU.max, negate=True).then_inc(sig[f"s_max{t}"], 1)

                def sums(s, t):
                    dve.wait_ge(sig[f"s_exp{t}"], s.n + 1)
                    dve.wait_ge(sig[f"s_norm{t}"], s.n)
                    v.reciprocal(lrec[:, t, :], lsum[:, t, :]).then_inc(sig[f"s_rec{t}"], 1)

                def prob_copy(s, t, half):
                    dve.wait_ge(sig[f"pT_mm{t}{half}"], s.n + 1)
                    dve.wait_ge(sig["oT_mm0"] if t else sig["oT_mm1"], s.n + t)
                    v.tensor_copy(pT[:, 4 * half:4 * half + 4, :], pairs(f"pT_mm{t}{half}")).then_inc(sig[f"pT{t}{half}"], 1)

                def residual_attn(s):
                    dve.wait_ge(sig["wo_mm"], s.n + 1)
                    x = X[:, bass.ds(s.col, L)]
                    v.tensor_tensor(x, half("wo_mm"), x, ALU.add).then_inc(sig["x_attn"], 1)

                def shift(s):
                    dve.wait_ge(sig["x_attn"], s.n + 1)
                    dve.wait_ge(sig["c_dev"], s.n)
                    for rows, src, dst in shifted(s.col):
                        last = v.tensor_scalar(hs[rows, dst], X[rows, src], 1.0, None, ALU.mult)
                    last.then_inc(sig["c_shift"], 1)

                def c_deviation(s):
                    dve.wait_ge(sig["c_mean"], s.n + 1)
                    dve.wait_ge(sig["c_lo"], s.n)
                    v.tensor_tensor(dev[:], hs[:], half("c_mean"), ALU.subtract).then_inc(sig["c_dev"], 1)

                def c_square(s):
                    dve.wait_ge(sig["c_dev"], s.n + 1)
                    dve.wait_ge(sig["c_rstd"], s.n)
                    v.tensor_tensor(csq[:], dev[:], dev[:], ALU.mult).then_inc(sig["c_sq"], 1)

                def c_newton_a(s):
                    dve.wait_ge(sig["c_rstd"], s.n + 1)
                    dve.wait_ge(sig["c_aff"], s.n)
                    v.scalar_tensor_tensor(cnwt[:], half("c_var"), LN_EPS, crstd[:], ALU.add, ALU.mult).then_inc(sig["c_na"], 1)

                def c_newton_b(s):
                    dve.wait_ge(sig["c_na"], s.n + 1)
                    v.scalar_tensor_tensor(cnwt[:], cnwt[:], -0.5, crstd[:], ALU.mult, ALU.mult).then_inc(sig["c_nb"], 1)

                def c_newton_c(s):
                    dve.wait_ge(sig["c_nb"], s.n + 1)
                    v.scalar_tensor_tensor(cnwt[:], cnwt[:], 1.5, crstd[:], ALU.add, ALU.mult).then_inc(sig["c_nc"], 1)

                def c_normalised(s):
                    dve.wait_ge(sig["c_nc"], s.n + 1)
                    v.tensor_tensor(xn[:], cnwt[:], dev[:], ALU.mult).then_inc(sig["c_xn"], 1)

                def c_affine(s):
                    dve.wait_ge(sig["c_xn"], s.n + 1)
                    v.tensor_scalar(hn[:], xn[:], lvec[:, s.layer, 0:1], lvec[:, s.layer, 1:2],
                                    ALU.mult, ALU.add).then_inc(sig["c_aff"], 1)

                def c_low(s):
                    dve.wait_ge(sig["c_hi"], s.n + 1)
                    dve.wait_ge(sig["c_up2"], s.n)
                    v.tensor_tensor(f_lo[:], hn[:], f_hi[:].bitcast(F32), ALU.subtract).then_inc(sig["c_lo"], 1)

                def geglu(s, k):
                    m = CHUNKS[k][1]
                    dve.wait_ge(sig[f"c_gelu{k}"], s.n + 1)
                    dve.wait_ge(sig["c_down"], s.n)
                    v.scalar_tensor_tensor(act_[0:m, k, :], ps[0:m, BANK[f"c_up{k}"], L:2 * L], b1s[0:m, s.layer, 0, k:k + 1],
                                           gel[0:m, k, :], ALU.add, ALU.mult).then_inc(sig[f"c_act{k}"], 1)

                def residual_ffn(s):
                    dve.wait_ge(sig["c_down"], s.n + 1)
                    x = X[:, bass.ds(s.col, L)]
                    v.scalar_tensor_tensor(x, half("c_down"), lvec[:, s.layer, 2:3], x, ALU.add, ALU.add).then_inc(sig["x_ffn"], 1)

                if st[1].on: newton_a(st[1], 1)
                if st[1].on: newton_b(st[1], 1)
                if st[4].on: c_low(st[4])
                if st[1].on: newton_c(st[1], 1)
                if st[1].on: values(st[1], 0)
                if st[0].on: h_high(st[0])
                if st[1].on: normed(st[1], 1)
                if st[0].on: h_low(st[0])
                if st[3].on: residual_attn(st[3])
                if st[2].on: sums(st[2], 1)
                if st[2].on: mixed(st[2])
                if st[3].on: shift(st[3])
                if st[1].on: q_transposed(st[1], 0)
                if st[4].on: geglu(st[4], 1)
                if st[3].on: c_deviation(st[3])
                if st[3].on: c_square(st[3])
                if st[0].on: square_sums(st[0], 0)
                if st[4].on: geglu(st[4], 2)
                if st[0].on: clip(st[0], 0)
                if st[2].on: prob_copy(st[2], 0, 1)
                if st[4].on: geglu(st[4], 0)
                if st[0].on: newton_a(st[0], 0)
                if st[1].on: maxes(st[1], 0)
                if st[0].on: newton_b(st[0], 0)
                if st[0].on: newton_c(st[0], 0)
                if st[3].on: c_newton_a(st[3])
                if st[0].on: normed(st[0], 0)
                if st[3].on: c_newton_b(st[3])
                if st[1].on: q_transposed(st[1], 1)
                if st[1].on: k_transposed(st[1], 1)
                if st[3].on: c_newton_c(st[3])
                if st[4].on: residual_ffn(st[4])
                if st[3].on: c_normalised(st[3])
                if st[2].on: prob_copy(st[2], 1, 0)
                if st[0].on: square_sums(st[0], 1)
                if st[3].on: c_affine(st[3])
                if st[0].on: clip(st[0], 1)
                if st[1].on: maxes(st[1], 1)
                if st[1].on: sums(st[1], 0)
            layers(dve, step)
            dve.wait_ge(sig["x_ffn"], SEQS * DEPTH + 1)
            for b in range(SEQS):
                o = slice(L * b, L * b + L)
                v.scalar_tensor_tensor(X1[:, o], X[:, o], mod[:, 5, b:b + 1], X1[:, o], ALU.mult,
                                       ALU.add).then_inc(sig["o_comp"], 1)

        @block.gpsimd
        def _(pool):
            g = nc.gpsimd
            raise_once(pool, STEPPED["gpsimd"])
            pool.wait_ge(sig["consts_in"], 16 * N_CONST)
            pool.wait_ge(sig["w_in"], 16 * W_LOADS * DEPTH)
            for l in range(DEPTH):
                g.tensor_scalar(wq_hi[l][:], wq_raw[l], 1.0, None, ALU.mult)
                g.tensor_scalar(w1_hi[l][:], w1_raw[l], 1.0, None, ALU.mult).then_inc(sig["w_hi"], 1)
                for t in range(TILES):
                    g.tensor_tensor(rot[:, l, t, 0:2, :], tab[:, t, 0:2, :], qks[:, l], ALU.mult)
                    for j in range(2):
                        g.tensor_tensor(heads(rot[:, l, t, 2 + j, :], 2), heads(tab[:, t, 2 + j, :], 2),
                                        heads(qks[:, l, j, :], 2)[:, ::-1, :], ALU.mult)
                pool.wait_ge(sig["w_hi"], l + 1)
                g.tensor_tensor(wq_lo[l][:], wq_raw[l], wq_hi[l][:].bitcast(F32), ALU.subtract)
                g.tensor_tensor(w1_lo[l][:], w1_raw[l], w1_hi[l][:].bitcast(F32), ALU.subtract)\
                    .then_inc(sig["w_ready"], 1)

            def branch_step(A, Bs, C, Ds, E, F):
                if Ds.on:
                    pool.wait_ge(sig["b_scan"], Ds.n + 1)
                    pool.wait_ge(sig["b_gate"], Ds.n + 1)
                    pool.wait_ge(sig["b_dev1"], Ds.n)
                    g.tensor_tensor(B["g"], B["y"], B["gate"], ALU.mult).then_inc(sig["b_g"], 1)

            branch(pool, branch_step)
            pool.wait_ge(sig["w_ready"], DEPTH)

            def step(*st):
                def rotate_cos(s, t):
                    table = rot[:, s.layer, t]
                    pool.wait_ge(sig[f"qk_n{t}"], s.n + 1)
                    pool.wait_ge(sig[f"qT_mm{t}"], s.n)
                    pool.wait_ge(sig[f"kT_mm{t}"], s.n)
                    for j in range(2):
                        o = slice(INNER * j, INNER * j + INNER)
                        last = g.tensor_tensor(heads(qk_u[:, t, o], HEADS), heads(qk_n[:, t, o], HEADS),
                                               table[:, j, :].unsqueeze(1).broadcast_to([128, HEADS, DH]), ALU.mult)
                    last.then_inc(sig[f"rot_u{t}"], 1)

                def rotate_sin(s, t):
                    table = rot[:, s.layer, t]
                    pool.wait_ge(sig[f"qk_n{t}"], s.n + 1)
                    pool.wait_ge(sig["rot0"] if t else sig["rot1"], s.n + t)
                    for j in range(2):
                        o = slice(INNER * j, INNER * j + INNER)
                        for half in range(2):
                            a, b = slice(32 * half, 32 * half + 32), slice(32 - 32 * half, 64 - 32 * half)
                            last = g.tensor_tensor(heads(qk_w[:, o], HEADS)[:, :, a], heads(qk_n[:, t, o], HEADS)[:, :, b],
                                                   table[:, 2 + j, a].unsqueeze(1).broadcast_to([128, HEADS, 32]), ALU.mult)
                    last.then_inc(sig[f"rot_w{t}"], 1)

                def rotate_add(s, t):
                    pool.wait_ge(sig[f"rot_u{t}"], s.n + 1)
                    pool.wait_ge(sig[f"rot_w{t}"], s.n + 1)
                    g.tensor_tensor(qk_u[:, t, :], qk_u[:, t, :], qk_w[:], ALU.add).then_inc(sig[f"rot{t}"], 1)

                def normalise(s, t):
                    pool.wait_ge(sig[f"s_rec{t}"], s.n + 1)
                    g.tensor_tensor(prob[:, t], prob[:, t], lrec[:, t, :].unsqueeze(2).broadcast_to([128, HEADS, 128]),
                                    ALU.mult).then_inc(sig[f"s_norm{t}"], 1)

                if st[1].on: rotate_sin(st[1], 0)
                if st[1].on: rotate_cos(st[1], 0)
                if st[1].on: rotate_add(st[1], 0)
                if st[2].on: normalise(st[2], 0)
                if st[1].on: rotate_sin(st[1], 1)
                if st[1].on: rotate_cos(st[1], 1)
                if st[2].on: normalise(st[2], 1)
                if st[1].on: rotate_add(st[1], 1)
            layers(pool, step)


def kernel(**inputs):
    import numpy as np
    import ml_dtypes
    import concourse.bacc as bacc
    from concourse.bass_utils import run_bass_kernel_spmd

    def t(name):
        return np.asarray(inputs[name])

    half = np.arange(0, DH, 2, dtype=np.float32)
    freqs = np.arange(L, dtype=np.float32)[:, None] * (1.0 / 10000.0 ** (half / DH)).astype(np.float32)[None, :]
    base = (half + 0.4 * DH) / (1.4 * DH)
    scale = base[None, :] ** ((np.arange(L) - L // 2) / float(WIN // 2))[:, None]
    cos, sin, scale = (np.concatenate([a, a], -1) for a in (np.cos(freqs), np.sin(freqs), scale))
    sin = sin * np.where(np.arange(DH) < DH // 2, -1.0, 1.0)[None, :]
    rot_tab = np.stack([8.0 * cos * scale, cos / scale, 8.0 * sin * scale, sin / scale], 1).astype(np.float32)
    rot_tab = rot_tab.reshape(TILES, 128, 4, DH).transpose(1, 0, 2, 3)
    row, slot = np.arange(128)[:, None], np.arange(128)[None, :]
    keys = np.stack([np.broadcast_to(slot, (128, 128)),
                     np.where((row < 64) & (slot >= 64), slot, slot + 128)])
    query = np.stack([np.broadcast_to(row, (128, 128)), np.broadcast_to(row + 128, (128, 128))])
    seen = (keys <= query) & (query <= keys + WIN)
    mask = np.where(seen, 0.0, -1e30).transpose(1, 0, 2)
    mask = np.tile(mask, (1, 1, 4)).astype(ml_dtypes.bfloat16)

    arrays = {
        "xT": t("L0_attn_x").reshape(TOK, D).T, "cT": t("L0_c").T, "wmod": t("L0_wmod"),
        "w_inT": t("L0_attn_W_in").T, "w_x0": t("L0_attn_W_x")[0:1], "w_dt": t("L0_attn_W_dt").reshape(1, D),
        "b_dt": t("L0_attn_b_dt").reshape(D, 1), "gamma": t("L0_attn_gamma").reshape(D, 1),
        "beta": t("L0_attn_beta").reshape(D, 1),
        "wqkv": t("L0_ffn_wqkv"), "q_scale": t("L0_ffn_q_scale"), "k_scale": t("L0_ffn_k_scale"),
        "wo": t("L0_ffn_wo"), "ln_g": t("L0_ffn_ln_g"), "ln_b": t("L0_ffn_ln_b"), "w1": t("L0_ffn_w1"),
        "b1": t("L0_ffn_b1"), "w2": t("L0_ffn_w2"), "b2": t("L0_ffn_b2"),
        "rot_tab": rot_tab, "mask": mask, "ident_bf": np.eye(128, dtype=ml_dtypes.bfloat16),
        "ident": np.eye(128, dtype=np.float32),
    }
    nc = bacc.Bacc("TRN2", target_bir_lowering=False, num_devices=1)
    feeds, args = {}, {}
    for name, a in arrays.items():
        a = np.ascontiguousarray(a)
        feeds[f"in_{name}"] = a
        args[name] = nc.dram_tensor(f"in_{name}", a.shape, mybir.dt.from_np(a.dtype), kind="ExternalInput").ap()
    args["outT"] = nc.dram_tensor("outT", (D, TOK), F32, kind="ExternalOutput").ap()
    build(nc, **args)
    r = run_bass_kernel_spmd(nc, [feeds], core_ids=[0])
    return np.ascontiguousarray(r.results[0]["outT"].T).reshape(SEQS, L, D)
```

```python
from contextlib import ExitStack

import concourse.bass as bass
from concourse import mybir

ALU = mybir.AluOpType
ACT = mybir.ActivationFunctionType
F32 = mybir.dt.float32
F32R = mybir.dt.float32r
BF16 = mybir.dt.bfloat16
AX = mybir.AxisListType

D = 128
SEQS = 32
L = 256
TOK = SEQS * L
TILES = L // 128
DEPTH = 2
HEADS = 8
DH = 64
INNER = HEADS * DH
PAIRS = HEADS // 2
HID = 341
CHUNKS = [(0, 128), (128, 128), (256, HID - 256)]
WIN = 64
LN_EPS = 1e-5
B_STAGES = 6
STAGES = 6
STEP = 512
STEPS = TOK // STEP
LN2 = 0.6931471805599453
NORM_SHIFT = 20
W_LOADS = 3 + 3 * 3 + 2 + 3

ONCE = (
    "c_in consts_in tables_in x_first x_rest w_in mod_in consts_set silu_sig silu_done mod_mm mod_gate outer_mm "
    "outer_set w_hi w_ready o_comp o_st"
).split()
STEPPED = {
    "tensor": (
        "b_mean0 b_mean1 b_mean2 b_var0 b_var1 b_var2 b_x b_z b_dtmm q_proj0 q_proj1 v_proj0 v_proj1 "
        "qT_mm0 qT_mm1 kT_mm0 kT_mm1 s_mm0 s_mm1 pT_mm00 pT_mm01 pT_mm10 pT_mm11 oT_mm0 oT_mm1 wo_mm "
        "c_mean c_var c_up0 c_up1 c_up2 c_down").split(),
    "scalar": (
        "b_sq1 b_sq2 b_ln0 b_ln1 b_ln2 b_rstd0 b_rstd1 b_rstd2 b_tanh b_gate b_dt b_decay qk_sq0 qk_sq1 "
        "v_sb0 v_sb1 qk_ln0 qk_ln1 qk_r0 qk_r1 qT0 qT1 kT0 s_exp0 s_exp1 pT01 pT10 pT11 oT0 oT1 c_sq "
        "c_ln c_rstd c_hi c_gelu0 c_gelu1 c_gelu2").split(),
    "vector": (
        "b_dev0 b_dev1 b_dev2 b_sq0 b_xn0 b_xn1 b_xn2 b_h b_xh b_a b_w b_scan b_g b_lng b_x1 b_hB h_hi "
        "h_lo v_mix qk_ss0 qk_ss1 qk_clip0 qk_clip1 qk_na0 qk_na1 qk_nb0 qk_nb1 qk_nc0 qk_nc1 qk_n0 "
        "qk_n1 kT1 s_max0 s_max1 s_rec0 s_rec1 s_norm1 pT00 o_lo0 o_lo1 x_attn c_shift c_dev c_na c_nb "
        "c_nc c_xn c_aff c_lo c_act0 c_act1 c_act2 x_ffn").split(),
    "gpsimd": (
        "rot_u0 rot_u1 rot_w0 rot_w1 rot0 rot1 s_norm0").split(),
}


class Signals:

    def __init__(self, nc, ctx):
        names = ONCE + [n for group in STEPPED.values() for n in group]
        self.by_name = {n: ctx.enter_context(nc.semaphore(n)) for n in names}

    def __getitem__(self, name):
        return self.by_name[name]


class Stage:

    def __init__(self, on, n, col, item, par, layer):
        self.on, self.n, self.col, self.item, self.par, self.layer = on, n, col, item, par, layer
        self.done = n + 1 if on else n


def pipeline(eng, depth, items, rounds, unroll, width, step):

    def fixed(m):
        st = []
        for k in range(depth):
            q = m - k
            on = 0 <= q < items * rounds
            b = q % items
            st.append(Stage(on, min(max(q, 0), items * rounds) + 1, b * width, b, q % 2, q // items))
        step(*st)

    lead = depth - 1 + (items - depth + 1) % unroll
    for r in range(rounds):
        for m in range(lead):
            fixed(r * items + m)
        with eng.Fori(0, (items - lead) // unroll) as i:
            for s in range(unroll):
                st = []
                for k in range(depth):
                    b = eng.snap(i * unroll + (lead + s - k))
                    st.append(Stage(True, eng.snap(b + (r * items + 1)), eng.snap(b * width), b,
                                    (lead + s - k) % 2, r))
                step(*st)
    for m in range(depth - 1):
        fixed(rounds * items + m)


def build(nc, xT, cT, wmod, w_inT, w_x0, w_dt, b_dt, gamma, beta, wqkv, q_scale, k_scale, wo,
          ln_g, ln_b, w1, b1, w2, b2, rot_tab, mask, ident_bf, ident, outT):
    with ExitStack() as ctx:
        def sb(name, shape, dt=F32):
            return ctx.enter_context(nc.sbuf_tensor(name, shape, dt))

        sig = Signals(nc, ctx)
        ps = ctx.enter_context(nc.psum_tensor("ps", [128, 8, 512], F32))
        BANK = {"q_proj0": 0, "q_proj1": 0, "v_proj0": 2, "v_proj1": 6, "qT_mm0": 4, "qT_mm1": 3,
            "kT_mm0": 6, "kT_mm1": 6, "s_mm0": 4, "s_mm1": 4, "pT_mm00": 7, "pT_mm01": 6,
            "pT_mm10": 3, "pT_mm11": 7, "oT_mm0": 2, "oT_mm1": 7, "wo_mm": 3, "c_mean": 5,
            "c_var": 6, "c_up0": 7, "c_up1": 2, "c_up2": 3, "c_down": 6}
        B_BANK = {"b_mean0": 3, "b_mean1": 6, "b_mean2": 2, "b_var0": 7, "b_var1": 6, "b_var2": 0,
            "b_x": 1, "b_z": 5, "b_dtmm": 4}
        BX, BZ = 6, 7

        X = sb("X", [128, TOK])
        X1 = sb("X1", [128, TOK])
        idf = sb("idf", [128, 128])
        idb = sb("idb", [128, 128], BF16)
        avg = sb("avg", [128, 128])
        maskb = sb("maskb", [128, TILES, 512], BF16)
        tab = sb("tab", [128, TILES, 4, DH])
        rot = sb("rot", [128, DEPTH, TILES, 4, DH])
        qks = sb("qks", [128, DEPTH, 2, DH])
        biases = sb("biases", [128, 3])
        cTs = sb("cTs", [128, SEQS])
        csig = sb("csig", [128, SEQS])
        csilu = sb("csilu", [128, SEQS])
        mod = sb("mod", [128, 6, SEQS])
        gsgn = sb("gsgn", [128, 2, SEQS])
        gabs = sb("gabs", [128, 2, SEQS])
        winT = sb("winT", [128, 2 * D])
        wx = sb("wx", [1, D])
        wdt = sb("wdt", [1, D])
        wouter = sb("wouter", [128, D])
        vec = sb("vec", [128, 3])
        wq_hi = [sb(f"wq_hi{l}", [128, 3 * INNER], F32R) for l in range(DEPTH)]
        wq_lo = [sb(f"wq_lo{l}", [128, 3 * INNER], F32R) for l in range(DEPTH)]
        w1_hi = [sb(f"w1_hi{l}", [128, 2 * HID], F32R) for l in range(DEPTH)]
        w1_lo = [sb(f"w1_lo{l}", [128, 2 * HID], F32R) for l in range(DEPTH)]
        wo_hi = [sb(f"wo_hi{l}", [128, PAIRS, D], F32R) for l in range(DEPTH)]
        wo_lo = [sb(f"wo_lo{l}", [128, PAIRS, D], F32R) for l in range(DEPTH)]
        w2s = sb("w2s", [128, DEPTH, 3, D])
        lvec = sb("lvec", [128, DEPTH, 3])
        b1s = sb("b1s", [128, DEPTH, 2, 3])
        h_hi = sb("h_hi_t", [128, L], F32R)
        h_lo = sb("h_lo_t", [128, L], F32R)
        qk_sq = sb("qk_sq", [128, 2 * INNER])
        ss = sb("ss", [128, TILES, 2 * HEADS])
        lnss = sb("lnss", [128, TILES, 2 * HEADS])
        rn = sb("rn", [128, TILES, 2 * HEADS])
        nwt = sb("nwt", [128, TILES, 2 * HEADS])
        qk_n = sb("qk_n", [128, TILES, 2 * INNER])
        qk_u = sb("qk_u", [128, TILES, 2 * INNER])
        qk_w = sb("qk_w", [128, 2 * INNER])
        V = sb("V", [128, 2, TILES + 1, INNER])
        qT = sb("qT_t", [128, PAIRS, L])
        kT = sb("kT_t", [128, PAIRS, L])
        nmax = sb("nmax", [128, TILES, HEADS])
        lsum = sb("lsum", [128, TILES, HEADS])
        lrec = sb("lrec", [128, TILES, HEADS])
        prob = sb("prob", [128, TILES, HEADS, 128])
        pT = sb("pT_t", [128, HEADS, 128])
        oT = sb("oT_t", [128, PAIRS, L], F32R)
        oT_lo = sb("oT_lo_t", [128, PAIRS, L], F32R)
        hs = sb("hs", [128, L])
        c_work = sb("c_work", [128, 4, L])
        dev, csq, crstd, cnwt = (c_work[:, i, :] for i in range(4))
        f_hi = sb("f_hi", [128, L], F32R)
        f_lo = sb("f_lo", [128, L], F32R)
        gel = sb("gel", [128, 3, L])
        act_ = sb("act_", [128, 3, L])
        cln, xn, hn = csq, cnwt, dev

        room = [t[:, c:c + 2, :].rearrange("p c k -> p (c k)") for t in (qT, kT) for c in (0, 2)]
        room += [c_work[:, c:c + 2, :].rearrange("p c k -> p (c k)") for c in (0, 2)]
        room += [V[:, p, t, :] for p in range(2) for t in range(3)]
        room += [prob[:, t, h:h + 4, :].rearrange("p h k -> p (h k)") for t in range(2) for h in (0, 4)]
        B = dict(zip("d0 d1 d2 sq0 sq1 sq2 r0 r1 r2 h tanh dt gate decay a".split(), room))
        B["w"] = pT[:, 0:4, :].rearrange("p h k -> p (h k)")
        B["y"] = pT[:, 4:8, :].rearrange("p h k -> p (h k)")
        B["g"] = gel[:, 0:2, :].rearrange("p h k -> p (h k)")
        B["ln1"] = act_[:, 0:2, :].rearrange("p h k -> p (h k)")
        wmods = X[:, 0:6 * D]
        flat = lambda t: t.rearrange("p t n -> p (t n)")
        wq_raw = [flat(qk_n[:])[:, 0:3 * INNER], flat(qk_u[:])[:, 0:3 * INNER]]
        wo_raw = [flat(qk_n[:])[:, 3 * INNER:], flat(qk_u[:])[:, 3 * INNER:]]
        w1_raw = [qk_w[:, 0:2 * HID], qk_sq[:, 0:2 * HID]]

        def heads(ap, n):
            return ap.rearrange("p (h d) -> p h d", h=n)

        def shifted(col):
            return ((slice(0, 64), bass.ds(col, L), slice(0, L)),
                    (slice(64, 128), bass.ds(col, L - 1), slice(1, L)))

        def raise_once(eng, names):
            for name in names:
                eng.sem_inc(sig[name], 1)

        def branch(eng, step):
            pipeline(eng, B_STAGES, STEPS, 1, 1, STEP, step)

        def layers(eng, step):
            pipeline(eng, STAGES, SEQS, DEPTH, 2, L, step)

        def two_before(eng, name, s):
            if not isinstance(s.n, int) or s.n > 2:
                eng.wait_ge(sig[name], s.n - 1)

        def full(name):
            return ps[:, BANK[name], :]

        def bfull(name):
            return ps[:, B_BANK[name], :]

        def halves(s):
            for b in range(2):
                yield slice(L * b, L * b + L), bass.ds(s.col + L * b, L), bass.ds(s.item * 2 + b, 1)

        def two(name):
            return ps[:, BANK[name]:BANK[name] + 2, :]

        def pairs(name):
            return ps[:, BANK[name], :].rearrange("p (c k) -> p c k", c=PAIRS)

        def half(name):
            return ps[:, BANK[name], 0:L]

        N_CONST, N_TABLES = 7, 4
        FIRST = 2 * STEP
        block = ctx.enter_context(nc.Block())

        @block.sync
        def _(sp):
            sp.dma_start(cTs[:], cT).then_inc(sig["c_in"], 16)
            for dst, src in ((wmods, wmod), (wx[:], w_x0), (wdt[:], w_dt), (vec[:, 0:1], b_dt),
                             (vec[:, 1:2], gamma), (vec[:, 2:3], beta), (winT[:], w_inT)):
                sp.dma_start(dst, src).then_inc(sig["consts_in"], 16)
            sp.dma_start(X1[:, 0:FIRST], xT[:, 0:FIRST]).then_inc(sig["x_first"], 16)
            sp.dma_start(X1[:, FIRST:], xT[:, FIRST:]).then_inc(sig["x_rest"], 16)
            for dst, src in ((tab[:], rot_tab), (idf[:], ident), (idb[:], ident_bf), (maskb[:], mask)):
                sp.dma_start(dst, src).then_inc(sig["tables_in"], 16)
            for l in range(DEPTH):
                loads = [(wq_raw[l], wqkv[l]), (w1_raw[l], w1[l]),
                         (wo_raw[l].rearrange("p (c n) -> p c n", c=PAIRS), wo[l].rearrange("(c p) n -> p c n", p=128)),
                         (qks[:, l, 0, :], q_scale[l:l + 1].broadcast_to([128, DH])),
                         (qks[:, l, 1, :], k_scale[l:l + 1].broadcast_to([128, DH]))]
                for c, (lo, n) in enumerate(CHUNKS):
                    loads.append((w2s[0:n, l, c, :], w2[l, lo:lo + n]))
                    for half in range(2):
                        o = half * HID + lo
                        loads.append((b1s[0:n, l, half, c:c + 1], b1[l:l + 1, o:o + n].rearrange("a p -> p a")))
                for c, v in enumerate((ln_g, ln_b, b2)):
                    loads.append((lvec[:, l, c:c + 1], v[l:l + 1].rearrange("a p -> p a")))
                assert len(loads) == W_LOADS
                for dst, src in loads:
                    sp.dma_start(dst, src).then_inc(sig["w_in"], 16)
            for b in range(0, SEQS, 4):
                sp.wait_ge(sig["o_comp"], b + 4)
                o = slice(b * L, (b + 4) * L)
                sp.dma_start(outT[:, o], X1[:, o]).then_inc(sig["o_st"], 16)
            sp.wait_ge(sig["o_st"], 16 * (SEQS // 4))

        @block.tensor
        def _(pe):
            mm = nc.tensor.matmul
            raise_once(pe, STEPPED["tensor"])
            pe.wait_ge(sig["silu_done"], 1)
            pe.wait_ge(sig["consts_in"], 16 * N_CONST)
            for j in range(6):
                last = mm(ps[:, BX, SEQS * j:SEQS * (j + 1)], wmods[:, D * j:D * (j + 1)], csilu[:],
                          start=True, stop=True)
            last.then_inc(sig["mod_mm"], 1)
            mm(ps[:, BZ, 0:D], wx[:], wdt[:], start=True, stop=True).then_inc(sig["outer_mm"], 1)
            pe.wait_ge(sig["outer_set"], 1)
            pe.wait_ge(sig["mod_gate"], 1)
            pe.wait_ge(sig["consts_set"], 1)
            pe.wait_ge(sig["x_first"], 16)

            def branch_step(*st):
                def mean(s, k):
                    if k == 0 and (not isinstance(s.item, int) or s.item >= FIRST // STEP):
                        pe.wait_ge(sig["x_rest"], 16)
                    if k:
                        pe.wait_ge(sig["b_g" if k == 1 else "b_x1"], s.n + 1)
                    src = B["g"] if k == 1 else X1[:, bass.ds(s.col, STEP)]
                    mm(bfull(f"b_mean{k}"), avg[:], src, start=True, stop=True).then_inc(sig[f"b_mean{k}"], 1)

                def variance(s, k):
                    pe.wait_ge(sig[f"b_sq{k}"], s.n + 1)
                    mm(bfull(f"b_var{k}"), avg[:], B[f"sq{k}"], start=True, stop=True).then_inc(sig[f"b_var{k}"], 1)

                def project_x(s):
                    pe.wait_ge(sig["b_h"], s.n + 1)
                    mm(bfull("b_x"), winT[:, 0:D], B["h"], start=True, stop=True).then_inc(sig["b_x"], 1)

                def project_z(s):
                    pe.wait_ge(sig["b_h"], s.n + 1)
                    mm(bfull("b_z"), winT[:, D:2 * D], B["h"], start=True, stop=True).then_inc(sig["b_z"], 1)

                def step_project(s):
                    pe.wait_ge(sig["b_tanh"], s.n + 1)
                    mm(bfull("b_dtmm"), wouter[:], B["tanh"], start=True, stop=True).then_inc(sig["b_dtmm"], 1)

                if st[0].on:
                    pe.wait_ge(sig["b_dev0"], st[0].n)
                    mean(st[0], 0)
                if st[4].on:
                    pe.wait_ge(sig["b_ln1"], st[4].n)
                    mean(st[4], 1)
                if st[2].on:
                    pe.wait_ge(sig["b_dt"], st[2].n)
                    step_project(st[2])
                if st[5].on:
                    pe.wait_ge(sig["b_dev2"], st[5].n)
                    mean(st[5], 2)
                if st[2].on:
                    pe.wait_ge(sig["b_gate"], st[2].n)
                    project_z(st[2])
                if st[4].on:
                    pe.wait_ge(sig["b_dev1"], st[4].done)
                    variance(st[4], 1)
                if st[5].on:
                    pe.wait_ge(sig["b_ln2"], st[5].n)
                    variance(st[5], 2)
                if st[0].on:
                    pe.wait_ge(sig["b_ln0"], st[0].n)
                    variance(st[0], 0)
                if st[1].on:
                    pe.wait_ge(sig["b_tanh"], st[1].n)
                    project_x(st[1])
            branch(pe, branch_step)
            pe.wait_ge(sig["w_ready"], DEPTH)
            pe.wait_ge(sig["tables_in"], 16 * N_TABLES)
            pe.wait_ge(sig["w_in"], 16 * W_LOADS * DEPTH)
            pe.wait_ge(sig["b_hB"], STEPS + 1)

            def step(*st):
                def q_k_project(s, t):
                    if t == 0:
                        pe.wait_ge(sig["h_hi"], s.n + 1)
                        pe.wait_ge(sig["h_lo"], s.n + 1)
                    tok = slice(128 * t, 128 * t + 128)
                    hi, lo = wq_hi[s.layer], wq_lo[s.layer]
                    for j in range(2):
                        o, dst = slice(INNER * j, INNER * j + INNER), ps[:, BANK[f"q_proj{t}"] + j, :]
                        mm(dst, h_hi[:, tok], lo[:, o], start=True, stop=False)
                        mm(dst, h_lo[:, tok], hi[:, o], start=False, stop=False)
                        last = mm(dst, h_hi[:, tok], hi[:, o], start=False, stop=True)
                    last.then_inc(sig[f"q_proj{t}"], 1)

                def v_project(s, t):
                    tok, o = slice(128 * t, 128 * t + 128), slice(2 * INNER, 3 * INNER)
                    hi, lo, dst = wq_hi[s.layer], wq_lo[s.layer], ps[:, BANK[f"v_proj{t}"], :]
                    mm(dst, h_hi[:, tok], lo[:, o], start=True, stop=False)
                    mm(dst, h_lo[:, tok], hi[:, o], start=False, stop=False)
                    mm(dst, h_hi[:, tok], hi[:, o], start=False, stop=True).then_inc(sig[f"v_proj{t}"], 1)

                def q_transpose(s, t):
                    pe.wait_ge(sig[f"rot{t}"], s.n + 1)
                    for c in range(PAIRS):
                        o = 128 * c
                        last = nc.tensor.transpose(ps[:, BANK[f"qT_mm{t}"], 128 * c:128 * c + 128], qk_u[:, t, o:o + 128], idf[:])
                    last.then_inc(sig[f"qT_mm{t}"], 1)

                def k_transpose(s, t):
                    pe.wait_ge(sig[f"rot{t}"], s.n + 1)
                    for c in range(PAIRS):
                        o = INNER + 128 * c
                        last = nc.tensor.transpose(ps[:, BANK[f"kT_mm{t}"], 128 * c:128 * c + 128], qk_u[:, t, o:o + 128], idf[:])
                    last.then_inc(sig[f"kT_mm{t}"], 1)

                def scores(s, t):
                    pe.wait_ge(sig[f"qT{t}"], s.n + 1)
                    pe.wait_ge(sig[f"kT{t}"], s.n + 1)
                    if t == 1:
                        pe.wait_ge(sig["kT0"], s.n + 1)
                    bank = BANK[f"s_mm{t}"]
                    for r in range(2):
                        mm(ps[:, bank + r, :], idb[:], maskb[:, t, :], start=True, stop=True)
                    for c in range(PAIRS):
                        o = slice(128 * c, 128 * c + 128)
                        if t == 0:
                            for w, r in ((0, 0), (1, 1), (0, 1), (1, 0)):
                                rows, n = slice(64 * r, 64 * r + 64), 64 * w + 64
                                last = mm(ps[64 * w:64 * w + 64, bank + r, 128 * c:128 * c + n],
                                          qT[rows, c, 64 * w:64 * w + 64], kT[rows, c, 0:n],
                                          start=False, stop=True, skip_group_check=True)
                        else:
                            for w, r in ((2, 0), (3, 1), (2, 1), (3, 0)):
                                rows = slice(64 * r, 64 * r + 64)
                                if w == 2:
                                    dst = ps[0:64, bank + r, o].rearrange("p (w k) -> p w k", w=2)
                                    keys = kT[rows, c, 64:192].rearrange("p (w k) -> p w k", w=2)[:, ::-1, :]
                                else:
                                    dst, keys = ps[64:128, bank + r, o], kT[rows, c, 128:256]
                                last = mm(dst, qT[rows, c, 64 * w:64 * w + 64], keys,
                                          start=False, stop=True, skip_group_check=True)
                    last.then_inc(sig[f"s_mm{t}"], 1)

                def prob_transpose(s, t, half):
                    pe.wait_ge(sig[f"s_norm{t}"], s.n + 1)
                    for j in range(4):
                        c, r = 2 * half + j // 2, j % 2
                        last = nc.tensor.transpose(ps[:, BANK[f"pT_mm{t}{half}"], 128 * j:128 * j + 128],
                                                   prob[:, t, 4 * r + c, :], idf[:])
                    last.then_inc(sig[f"pT_mm{t}{half}"], 1)

                def attend(s, t):
                    pe.wait_ge(sig["v_mix" if t else "v_sb0"], s.n + 1)
                    bank = BANK[f"oT_mm{t}"]
                    for half in range(2):
                        pe.wait_ge(sig[f"pT{t}{half}"], s.n + 1)
                        for j in range(4):
                            c, r = 2 * half + j // 2, j % 2
                            rows = slice(64 * r, 64 * r + 64)
                            feat = slice(DH * (2 * c + r), DH * (2 * c + r) + DH)
                            if t == 0:
                                last = mm(ps[rows, bank, 128 * c:128 * c + 128], V[:, s.par, 0, feat],
                                          pT[:, 2 * c + r, :], start=True, stop=True)
                            else:
                                mm(ps[rows, bank, 128 * c:128 * c + 64], V[:, s.par, TILES, feat],
                                   pT[:, 2 * c + r, 0:64], start=True, stop=True)
                                last = mm(ps[rows, bank, 128 * c + 64:128 * c + 128], V[:, s.par, 1, feat],
                                          pT[:, 2 * c + r, 64:128], start=True, stop=True)
                    last.then_inc(sig[f"oT_mm{t}"], 1)

                def out_proj(s):
                    for t in range(TILES):
                        pe.wait_ge(sig[f"o_lo{t}"], s.n + 1)
                    for c in range(PAIRS):
                        mm(half("wo_mm"), wo_lo[s.layer][:, c, :], oT[:, c, :], start=(c == 0), stop=False)
                        mm(half("wo_mm"), wo_hi[s.layer][:, c, :], oT_lo[:, c, :], start=False, stop=False)
                        last = mm(half("wo_mm"), wo_hi[s.layer][:, c, :], oT[:, c, :], start=False, stop=(c == PAIRS - 1))
                    last.then_inc(sig["wo_mm"], 1)

                def c_mean(s):
                    pe.wait_ge(sig["c_shift"], s.n + 1)
                    mm(half("c_mean"), avg[:], hs[:], start=True, stop=True).then_inc(sig["c_mean"], 1)

                def c_var(s):
                    pe.wait_ge(sig["c_sq"], s.n + 1)
                    mm(half("c_var"), avg[:], csq[:], start=True, stop=True).then_inc(sig["c_var"], 1)

                def c_up(s, k):
                    pe.wait_ge(sig["c_lo"], s.n + 1)
                    lo, m = CHUNKS[k]
                    hi_w, lo_w = w1_hi[s.layer], w1_lo[s.layer]
                    for value in range(2):
                        o = slice((1 - value) * HID + lo, (1 - value) * HID + lo + m)
                        dst = ps[0:m, BANK[f"c_up{k}"], value * L:value * L + L]
                        mm(dst, lo_w[:, o], f_hi[:], start=True, stop=False)
                        mm(dst, hi_w[:, o], f_lo[:], start=False, stop=False)
                        last = mm(dst, hi_w[:, o], f_hi[:], start=False, stop=True)
                    last.then_inc(sig[f"c_up{k}"], 1)

                def c_down(s):
                    for k, (lo, m) in enumerate(CHUNKS):
                        pe.wait_ge(sig[f"c_act{k}"], s.n + 1)
                        last = mm(half("c_down"), w2s[0:m, s.layer, k, :], act_[0:m, k, :], start=(k == 0), stop=(k == 2))
                    last.then_inc(sig["c_down"], 1)

                if st[1].on:
                    pe.wait_ge(sig["s_exp1"], st[1].n)
                    q_transpose(st[1], 0)
                if st[4].on:
                    pe.wait_ge(sig["pT00"], st[1].n)
                    if not st[1].on:
                        pe.wait_ge(sig["o_lo1"], st[2].n)
                        pe.wait_ge(sig["pT11"], st[2].n)
                        pe.wait_ge(sig["c_act0"], st[4].n)
                    c_up(st[4], 0)
                if st[0].on:
                    pe.wait_ge(sig["qk_n1"], st[0].n)
                    q_k_project(st[0], 0)
                if st[4].on:
                    pe.wait_ge(sig["o_lo0"], st[1].n)
                    if not st[1].on:
                        pe.wait_ge(sig["v_sb0"], st[0].n)
                        pe.wait_ge(sig["c_act1"], st[4].n)
                    c_up(st[4], 1)
                if st[3].on:
                    pe.wait_ge(sig["kT0"], st[0].n)
                    if not st[0].on:
                        pe.wait_ge(sig["x_ffn"], st[4].n)
                        pe.wait_ge(sig["pT01"], st[1].n)
                        pe.wait_ge(sig["v_sb1"], st[0].n)
                        pe.wait_ge(sig["kT1"], st[1].n)
                        pe.wait_ge(sig["c_na"], st[3].n)
                    c_var(st[3])
                if st[1].on:
                    pe.wait_ge(sig["qT0"], st[1].done)
                    pe.wait_ge(sig["c_dev"], st[2].n)
                    if not st[2].on:
                        pe.wait_ge(sig["s_exp1"], st[1].n)
                        pe.wait_ge(sig["s_exp0"], st[1].n)
                    scores(st[1], 0)
                if st[2].on:
                    pe.wait_ge(sig["c_act2"], st[3].n)
                    if not st[3].on:
                        pe.wait_ge(sig["x_attn"], st[2].n)
                        pe.wait_ge(sig["qT1"], st[1].n)
                        pe.wait_ge(sig["pT10"], st[2].n)
                    prob_transpose(st[2], 1, 0)
                if st[2].on:
                    pe.wait_ge(sig["c_act0"], st[4].done)
                    if not st[4].on:
                        pe.wait_ge(sig["pT00"], st[1].n)
                        pe.wait_ge(sig["o_lo1"], st[2].n)
                        pe.wait_ge(sig["pT11"], st[2].n)
                    prob_transpose(st[2], 1, 1)
                if st[0].on:
                    pe.wait_ge(sig["c_act1"], st[4].done)
                    if not st[4].on:
                        pe.wait_ge(sig["o_lo0"], st[1].n)
                        pe.wait_ge(sig["v_sb0"], st[0].n)
                    v_project(st[0], 0)
                if st[1].on:
                    pe.wait_ge(sig["pT10"], st[2].done)
                    if not st[2].on:
                        pe.wait_ge(sig["c_act2"], st[3].n)
                        pe.wait_ge(sig["x_attn"], st[2].n)
                        pe.wait_ge(sig["qT1"], st[1].n)
                    q_transpose(st[1], 1)
                if st[1].on:
                    pe.wait_ge(sig["c_na"], st[3].done)
                    if not st[3].on:
                        pe.wait_ge(sig["kT0"], st[0].n)
                        pe.wait_ge(sig["x_ffn"], st[4].n)
                        pe.wait_ge(sig["pT01"], st[1].n)
                        pe.wait_ge(sig["v_sb1"], st[0].n)
                        pe.wait_ge(sig["kT1"], st[1].n)
                    k_transpose(st[1], 1)
                if st[2].on:
                    pe.wait_ge(sig["pT11"], st[2].done)
                    attend(st[2], 1)
                if st[0].on:
                    pe.wait_ge(sig["qk_n0"], st[0].done)
                    q_k_project(st[0], 1)
                if st[0].on:
                    pe.wait_ge(sig["kT1"], st[1].done)
                    if not st[1].on:
                        pe.wait_ge(sig["c_na"], st[3].done)
                        pe.wait_ge(sig["kT0"], st[0].n)
                        pe.wait_ge(sig["x_ffn"], st[4].n)
                        pe.wait_ge(sig["pT01"], st[1].n)
                        pe.wait_ge(sig["v_sb1"], st[0].n)
                    v_project(st[0], 1)
                if st[1].on:
                    pe.wait_ge(sig["s_exp0"], st[1].done)
                    scores(st[1], 1)
                if st[1].on:
                    pe.wait_ge(sig["o_lo1"], st[2].done)
                    if not st[2].on:
                        pe.wait_ge(sig["pT11"], st[2].done)
                        pe.wait_ge(sig["c_act0"], st[4].done)
                        pe.wait_ge(sig["pT00"], st[1].n)
                    prob_transpose(st[1], 0, 0)
                if st[1].on:
                    pe.wait_ge(sig["v_sb1"], st[0].done)
                    if not st[0].on:
                        pe.wait_ge(sig["kT1"], st[1].done)
                        pe.wait_ge(sig["c_na"], st[3].done)
                        pe.wait_ge(sig["kT0"], st[0].n)
                        pe.wait_ge(sig["x_ffn"], st[4].n)
                        pe.wait_ge(sig["pT01"], st[1].n)
                    prob_transpose(st[1], 0, 1)
                if st[2].on:
                    pe.wait_ge(sig["qT1"], st[1].done)
                    if not st[1].on:
                        pe.wait_ge(sig["pT10"], st[2].done)
                        pe.wait_ge(sig["c_act2"], st[3].n)
                        pe.wait_ge(sig["x_attn"], st[2].n)
                    out_proj(st[2])
                if st[4].on:
                    pe.wait_ge(sig["pT01"], st[1].done)
                    if not st[1].on:
                        pe.wait_ge(sig["v_sb1"], st[0].done)
                        pe.wait_ge(sig["kT1"], st[1].done)
                        pe.wait_ge(sig["c_na"], st[3].done)
                        pe.wait_ge(sig["kT0"], st[0].n)
                        pe.wait_ge(sig["x_ffn"], st[4].n)
                    c_down(st[4])
                if st[1].on:
                    pe.wait_ge(sig["v_sb0"], st[0].done)
                    if not st[0].on:
                        pe.wait_ge(sig["c_act1"], st[4].done)
                        pe.wait_ge(sig["o_lo0"], st[1].n)
                    attend(st[1], 0)
                if st[3].on:
                    pe.wait_ge(sig["x_attn"], st[2].done)
                    if not st[2].on:
                        pe.wait_ge(sig["qT1"], st[1].done)
                        pe.wait_ge(sig["pT10"], st[2].done)
                        pe.wait_ge(sig["c_act2"], st[3].n)
                    c_up(st[3], 2)
                if st[2].on:
                    pe.wait_ge(sig["s_exp1"], st[1].done)
                    if not st[1].on:
                        pe.wait_ge(sig["s_exp0"], st[1].done)
                        pe.wait_ge(sig["c_dev"], st[2].n)
                    c_mean(st[2])
                if st[0].on:
                    pe.wait_ge(sig["x_ffn"], st[4].done)
                    if not st[4].on:
                        pe.wait_ge(sig["pT01"], st[1].done)
                        pe.wait_ge(sig["v_sb1"], st[0].done)
                        pe.wait_ge(sig["kT1"], st[1].done)
                        pe.wait_ge(sig["c_na"], st[3].done)
                        pe.wait_ge(sig["kT0"], st[0].n)
                    k_transpose(st[0], 0)
            layers(pe, step)

        @block.scalar
        def _(act):
            f = nc.scalar.activation
            raise_once(act, STEPPED["scalar"])
            act.wait_ge(sig["c_in"], 16)
            f(csig[:], cTs[:], ACT.Sigmoid).then_inc(sig["silu_sig"], 1)
            act.wait_ge(sig["consts_set"], 1)

            def branch_step(*st):
                def square(s, k):
                    act.wait_ge(sig[f"b_dev{k}"], s.n + 1)
                    act.wait_ge(sig[f"b_var{k}"], s.n)
                    f(B[f"sq{k}"], B[f"d{k}"], ACT.Square, scale=0.25 if k == 1 else 1.0).then_inc(sig[f"b_sq{k}"], 1)

                def logarithm(s, k):
                    act.wait_ge(sig[f"b_var{k}"], s.n + 1)
                    act.wait_ge(sig[("b_h", "b_lng", "b_hB")[k]], s.n)
                    f(B[f"r{k}"], bfull(f"b_var{k}"), ACT.Ln, bias=biases[:, 0:1]).then_inc(sig[f"b_ln{k}"], 1)

                def root(s, k):
                    act.wait_ge(sig[f"b_ln{k}"], s.n + 1)
                    f(B[f"r{k}"], B[f"r{k}"], ACT.Exp, scale=-0.5).then_inc(sig[f"b_rstd{k}"], 1)

                def tanh_x(s):
                    act.wait_ge(sig["b_x"], s.n + 1)
                    act.wait_ge(sig["b_w"], s.n)
                    act.wait_ge(sig["b_dtmm"], s.n)
                    f(B["tanh"], bfull("b_x"), ACT.Tanh).then_inc(sig["b_tanh"], 1)

                def tanh_z(s):
                    act.wait_ge(sig["b_z"], s.n + 1)
                    act.wait_ge(sig["b_g"], s.n)
                    f(B["gate"], bfull("b_z"), ACT.Tanh, scale=0.5).then_inc(sig["b_gate"], 1)

                def tanh_dt(s):
                    act.wait_ge(sig["b_dtmm"], s.n + 1)
                    act.wait_ge(sig["b_decay"], s.n)
                    f(B["dt"], bfull("b_dtmm"), ACT.Tanh, bias=vec[:, 0:1], scale=0.5).then_inc(sig["b_dt"], 1)

                def tanh_decay(s):
                    act.wait_ge(sig["b_dt"], s.n + 1)
                    act.wait_ge(sig["b_a"], s.n)
                    act.wait_ge(sig["b_w"], s.n)
                    f(B["decay"], B["dt"], ACT.Tanh, bias=biases[:, 2:3], scale=0.25).then_inc(sig["b_decay"], 1)

                if st[5].on: logarithm(st[5], 2)
                if st[0].on: logarithm(st[0], 0)
                act.preload_act_table_set("exp_and_others")
                if st[4].on: root(st[4], 1)
                if st[1].on: tanh_x(st[1])
                if st[0].on: root(st[0], 0)
                if st[2].on: tanh_z(st[2])
                if st[5].on: root(st[5], 2)
                if st[1].on: tanh_dt(st[1])
                if st[3].on: square(st[3], 1)
                if st[1].on: tanh_decay(st[1])
                if st[4].on: square(st[4], 2)
                act.preload_act_table_set("natural_log")
                if st[3].on: logarithm(st[3], 1)
            branch(act, branch_step)
            act.wait_ge(sig["w_in"], 16 * W_LOADS * DEPTH)
            act.wait_ge(sig["w_ready"], DEPTH)
            act.wait_ge(sig["b_hB"], STEPS + 1)

            def step(*st):
                def squares(s, t):
                    act.wait_ge(sig[f"q_proj{t}"], s.n + 1)
                    act.wait_ge(sig["qk_ss0"] if t else sig["qk_ss1"], s.n + t)
                    f(heads(qk_sq[:], 2), two(f"q_proj{t}"), ACT.Square).then_inc(sig[f"qk_sq{t}"], 1)

                def values(s, t):
                    act.wait_ge(sig[f"v_proj{t}"], s.n + 1)
                    two_before(act, f"oT_mm{t}", s)
                    two_before(act, "v_mix", s)
                    f(V[:, s.par, t, :], full(f"v_proj{t}"), ACT.Copy).then_inc(sig[f"v_sb{t}"], 1)

                def norm_ln(s, t):
                    act.wait_ge(sig[f"qk_clip{t}"], s.n + 1)
                    act.wait_ge(sig[f"qk_r{t}"], s.n)
                    f(lnss[:, t, :], ss[:, t, :], ACT.Ln, scale=float(2 ** NORM_SHIFT)).then_inc(sig[f"qk_ln{t}"], 1)

                def norm_exp(s, t):
                    act.wait_ge(sig[f"qk_ln{t}"], s.n + 1)
                    act.wait_ge(sig[f"qk_n{t}"], s.n)
                    f(rn[:, t, :], lnss[:, t, :], ACT.Exp, scale=-0.5, bias=biases[:, 1:2]).then_inc(sig[f"qk_r{t}"], 1)

                def q_transposed(s, t):
                    act.wait_ge(sig[f"qT_mm{t}"], s.n + 1)
                    act.wait_ge(sig[f"s_mm{t}"], s.n)
                    f(qT[:, :, 128 * t:128 * t + 128], pairs(f"qT_mm{t}"), ACT.Copy).then_inc(sig[f"qT{t}"], 1)

                def k_transposed(s, t):
                    act.wait_ge(sig[f"kT_mm{t}"], s.n + 1)
                    act.wait_ge(sig["s_mm0"], s.n)
                    act.wait_ge(sig["s_mm1"], s.n)
                    f(kT[:, :, 128 * t:128 * t + 128], pairs(f"kT_mm{t}"), ACT.Copy).then_inc(sig[f"kT{t}"], 1)

                def exps(s, t):
                    act.wait_ge(sig[f"s_max{t}"], s.n + 1)
                    act.wait_ge(sig["pT_mm11"] if t else sig["pT_mm01"], s.n)
                    act.wait_ge(sig[f"s_rec{t}"], s.n)
                    for h in range(HEADS):
                        o = slice(128 * (h % 4), 128 * (h % 4) + 128)
                        last = f(prob[:, t, h, :], ps[:, BANK[f"s_mm{t}"] + h // 4, o], ACT.Exp,
                                 bias=nmax[:, t, h:h + 1], accum_out=lsum[:, t, h:h + 1])
                    last.then_inc(sig[f"s_exp{t}"], 1)

                def prob_copy(s, t, half):
                    act.wait_ge(sig[f"pT_mm{t}{half}"], s.n + 1)
                    act.wait_ge(sig["oT_mm0"] if t else sig["oT_mm1"], s.n + t)
                    f(pT[:, 4 * half:4 * half + 4, :], pairs(f"pT_mm{t}{half}"), ACT.Copy).then_inc(sig[f"pT{t}{half}"], 1)

                def attended(s, t):
                    act.wait_ge(sig[f"oT_mm{t}"], s.n + 1)
                    act.wait_ge(sig["wo_mm"], s.n)
                    act.wait_ge(sig[f"o_lo{t}"], s.n)
                    f(oT[:, :, 128 * t:128 * t + 128], pairs(f"oT_mm{t}"), ACT.Copy).then_inc(sig[f"oT{t}"], 1)

                def c_square(s):
                    act.wait_ge(sig["c_dev"], s.n + 1)
                    act.wait_ge(sig["c_rstd"], s.n)
                    f(csq[:], dev[:], ACT.Square).then_inc(sig["c_sq"], 1)

                def c_logarithm(s):
                    act.wait_ge(sig["c_var"], s.n + 1)
                    f(cln[:], half("c_var"), ACT.Ln, bias=biases[:, 0:1]).then_inc(sig["c_ln"], 1)

                def c_root(s):
                    act.wait_ge(sig["c_ln"], s.n + 1)
                    act.wait_ge(sig["c_nc"], s.n)
                    f(crstd[:], cln[:], ACT.Exp, scale=-0.5).then_inc(sig["c_rstd"], 1)

                def c_high(s):
                    act.wait_ge(sig["c_aff"], s.n + 1)
                    act.wait_ge(sig["c_up1"], s.n)
                    act.wait_ge(sig["c_lo"], s.n)
                    f(f_hi[:], hn[:], ACT.Copy).then_inc(sig["c_hi"], 1)

                def gelu(s, k):
                    m = CHUNKS[k][1]
                    act.wait_ge(sig[f"c_up{k}"], s.n + 1)
                    act.wait_ge(sig[f"c_act{k}"], s.n)
                    f(gel[0:m, k, :], ps[0:m, BANK[f"c_up{k}"], 0:L], ACT.Gelu,
                      bias=b1s[0:m, s.layer, 1, k:k + 1]).then_inc(sig[f"c_gelu{k}"], 1)

                if st[1].on: k_transposed(st[1], 0)
                if st[3].on: c_square(st[3])
                if st[1].on: q_transposed(st[1], 0)
                if st[4].on: gelu(st[4], 0)
                if st[0].on: squares(st[0], 0)
                if st[4].on: gelu(st[4], 1)
                act.preload_act_table_set("natural_log_exp_and_others")
                if st[3].on: c_logarithm(st[3])
                if st[0].on: norm_ln(st[0], 0)
                if st[3].on: c_root(st[3])
                if st[0].on: norm_exp(st[0], 0)
                if st[2].on: prob_copy(st[2], 1, 0)
                if st[2].on: prob_copy(st[2], 1, 1)
                if st[1].on: exps(st[1], 0)
                if st[1].on: q_transposed(st[1], 1)
                if st[2].on: attended(st[2], 1)
                if st[0].on: squares(st[0], 1)
                if st[0].on: values(st[0], 1)
                if st[0].on: values(st[0], 0)
                if st[0].on: norm_ln(st[0], 1)
                if st[3].on: c_high(st[3])
                if st[0].on: norm_exp(st[0], 1)
                if st[1].on: prob_copy(st[1], 0, 1)
                if st[1].on: exps(st[1], 1)
                if st[1].on: attended(st[1], 0)
                act.preload_act_table_set("gelu_and_others")
                if st[3].on: gelu(st[3], 2)
            layers(act, step)

        @block.vector
        def _(dve):
            v = nc.vector
            raise_once(dve, STEPPED["vector"])
            v.memset(avg[:], 1.0 / D)
            v.memset(biases[:, 0:1], LN_EPS)
            v.memset(biases[:, 1:2], NORM_SHIFT / 2 * LN2)
            v.memset(biases[:, 2:3], 0.25)
            v.memset(h_hi[64:128, 0:1].bitcast(F32), 0.0)
            v.memset(h_lo[64:128, 0:1].bitcast(F32), 0.0)
            v.memset(hs[64:128, 0:1], 0.0).then_inc(sig["consts_set"], 1)
            dve.wait_ge(sig["silu_sig"], 1)
            v.tensor_tensor(csilu[:], cTs[:], csig[:], ALU.mult).then_inc(sig["silu_done"], 1)
            dve.wait_ge(sig["mod_mm"], 1)
            modp = ps[:, BX, 0:6 * SEQS].rearrange("p (j b) -> p j b", j=6)
            for j in range(6):
                v.tensor_scalar(mod[:, j, :], modp[:, j, :], 1.0 if j in (1, 4) else 0.0, None, ALU.add)
            dve.wait_ge(sig["outer_mm"], 1)
            v.tensor_copy(wouter[:], ps[:, BZ, 0:D]).then_inc(sig["outer_set"], 1)
            v.tensor_scalar(vec[:, 0:1], vec[:, 0:1], 0.5, None, ALU.mult)
            v.tensor_scalar(vec[:, 1:2], vec[:, 1:2], 0.25, None, ALU.mult)
            for s, j in enumerate((2, 5)):
                last = v.tensor_scalar(gsgn[:, s, :], modp[:, j, :], 0.0, 2.0, ALU.is_ge, ALU.mult)
            last.then_inc(sig["mod_in"], 1)
            dve.wait_ge(sig["mod_in"], 1)
            for s, j in enumerate((2, 5)):
                last = v.scalar_tensor_tensor(gabs[:, s, :], modp[:, j, :], -1.0, mod[:, j, :], ALU.mult, ALU.max)
            last.then_inc(sig["mod_in"], 1)
            dve.wait_ge(sig["mod_in"], 2)
            v.tensor_scalar(gabs[:], gabs[:], 0.25, None, ALU.max).then_inc(sig["mod_in"], 1)
            dve.wait_ge(sig["mod_in"], 3)
            for s, j in enumerate((2, 5)):
                last = v.scalar_tensor_tensor(mod[:, j, :], gsgn[:, s, :], -1.0, gabs[:, s, :], ALU.add, ALU.mult)
            last.then_inc(sig["mod_gate"], 1)
            dve.wait_ge(sig["mod_gate"], 1)

            def branch_step(*st):
                def deviation(s, k):
                    dve.wait_ge(sig[f"b_mean{k}"], s.n + 1)
                    dve.wait_ge(sig[f"b_xn{k}"], s.n)
                    dve.wait_ge(sig[f"b_sq{k}"], s.n)
                    src = B["g"] if k == 1 else X1[:, bass.ds(s.col, STEP)]
                    v.tensor_tensor(B[f"d{k}"], src, bfull(f"b_mean{k}"), ALU.subtract).then_inc(sig[f"b_dev{k}"], 1)

                def square(s, k):
                    dve.wait_ge(sig[f"b_dev{k}"], s.n + 1)
                    dve.wait_ge(sig[f"b_var{k}"], s.n)
                    v.scalar_tensor_tensor(B[f"sq{k}"], B[f"d{k}"], 0.0625 if k == 1 else 1.0, B[f"d{k}"], ALU.mult, ALU.mult).then_inc(sig[f"b_sq{k}"], 1)

                def normalised(s, k):
                    dve.wait_ge(sig[f"b_rstd{k}"], s.n + 1)
                    dve.wait_ge(sig[f"b_dev{k}"], s.n + 1)
                    v.tensor_tensor(B[f"r{k}"], B[f"d{k}"], B[f"r{k}"], ALU.mult).then_inc(sig[f"b_xn{k}"], 1)

                def modulated(s):
                    dve.wait_ge(sig["b_xn0"], s.n + 1)
                    dve.wait_ge(sig["b_x"], s.n)
                    dve.wait_ge(sig["b_z"], s.n)
                    dve.wait_ge(sig["b_xh"], s.n)
                    for o, _, b in halves(s):
                        last = v.tensor_scalar(B["h"][:, o], B["r0"][:, o], mod[:, 1, b], mod[:, 0, b], ALU.mult, ALU.add)
                    last.then_inc(sig["b_h"], 1)

                def residual_h(s):
                    dve.wait_ge(sig["b_h"], s.n + 1)
                    dve.wait_ge(sig["b_dev0"], s.n + 1)
                    for o, cols, b in halves(s):
                        last = v.scalar_tensor_tensor(X1[:, cols], B["h"][:, o], mod[:, 2, b], X1[:, cols], ALU.mult, ALU.add)
                    last.then_inc(sig["b_xh"], 1)

                def decayed(s):
                    dve.wait_ge(sig["b_decay"], s.n + 1)
                    dve.wait_ge(sig["b_scan"], s.n)
                    v.tensor_scalar(B["a"], B["decay"], -0.5, 0.5, ALU.mult, ALU.add).then_inc(sig["b_a"], 1)

                def scan_input(s):
                    dve.wait_ge(sig["b_decay"], s.n + 1)
                    dve.wait_ge(sig["b_scan"], s.n)
                    v.scalar_tensor_tensor(B["w"], B["decay"], 1.0, B["tanh"], ALU.add, ALU.mult).then_inc(sig["b_w"], 1)

                def scan(s):
                    dve.wait_ge(sig["b_w"], s.n + 1)
                    dve.wait_ge(sig["b_a"], s.n + 1)
                    dve.wait_ge(sig["b_g"], s.n)
                    for o, _, _ in halves(s):
                        last = v.tensor_tensor_scan(B["y"][:, o], B["a"][:, o], B["w"][:, o], 0.0, ALU.mult, ALU.add)
                    last.then_inc(sig["b_scan"], 1)

                def gated(s):
                    dve.wait_ge(sig["b_scan"], s.n + 1)
                    dve.wait_ge(sig["b_gate"], s.n + 1)
                    dve.wait_ge(sig["b_dev1"], s.n)
                    v.scalar_tensor_tensor(B["g"], B["gate"], 1.0, B["y"], ALU.add, ALU.mult).then_inc(sig["b_g"], 1)

                def affine(s):
                    dve.wait_ge(sig["b_xn1"], s.n + 1)
                    dve.wait_ge(sig["b_x1"], s.n)
                    v.tensor_scalar(B["ln1"], B["r1"], vec[:, 1:2], vec[:, 2:3], ALU.mult, ALU.add).then_inc(sig["b_lng"], 1)

                def residual_norm(s):
                    dve.wait_ge(sig["b_lng"], s.n + 1)
                    dve.wait_ge(sig["b_xh"], s.n + 1)
                    for o, cols, b in halves(s):
                        last = v.scalar_tensor_tensor(X1[:, cols], B["ln1"][:, o], mod[:, 2, b], X1[:, cols], ALU.mult, ALU.add)
                    last.then_inc(sig["b_x1"], 1)

                def layers_input(s):
                    dve.wait_ge(sig["b_xn2"], s.n + 1)
                    for o, cols, b in halves(s):
                        last = v.tensor_scalar(X[:, cols], B["r2"][:, o], mod[:, 4, b], mod[:, 3, b], ALU.mult, ALU.add)
                    last.then_inc(sig["b_hB"], 1)

                if st[0].on: deviation(st[0], 0)
                if st[0].on: square(st[0], 0)
                if st[1].on: modulated(st[1])
                if st[2].on: decayed(st[2])
                if st[2].on: scan_input(st[2])
                if st[3].on: gated(st[3])
                if st[1].on: residual_h(st[1])
                if st[2].on: scan(st[2])
                if st[4].on: normalised(st[4], 1)
                if st[4].on: affine(st[4])
                if st[4].on: residual_norm(st[4])
                if st[3].on: deviation(st[3], 1)
                if st[5].on: normalised(st[5], 2)
                if st[0].on: normalised(st[0], 0)
                if st[4].on: deviation(st[4], 2)
                if st[5].on: layers_input(st[5])
            branch(dve, branch_step)
            dve.wait_ge(sig["b_hB"], STEPS + 1)
            dve.wait_ge(sig["w_ready"], DEPTH)

            def step(*st):
                def h_high(s):
                    if s.layer:
                        dve.wait_ge(sig["x_ffn"], s.n - SEQS + 1)
                    dve.wait_ge(sig["v_proj1"], s.n)
                    dve.wait_ge(sig["h_lo"], s.n)
                    for rows, src, dst in shifted(s.col):
                        last = v.tensor_scalar(h_hi[rows, dst], X[rows, src], 1.0, None, ALU.mult)
                    last.then_inc(sig["h_hi"], 1)

                def h_low(s):
                    dve.wait_ge(sig["h_hi"], s.n + 1)
                    dve.wait_ge(sig["v_proj1"], s.n)
                    for rows, src, dst in shifted(s.col):
                        last = v.tensor_tensor(h_lo[rows, dst], X[rows, src], h_hi[rows, dst].bitcast(F32), ALU.subtract)
                    last.then_inc(sig["h_lo"], 1)

                def mixed(s):
                    dve.wait_ge(sig["v_sb0"], s.n + 1)
                    dve.wait_ge(sig["v_sb1"], s.n + 1)
                    two_before(dve, "oT_mm1", s)
                    v.tensor_copy(V[0:64, s.par, TILES, :], V[0:64, s.par, 1, :])
                    v.tensor_copy(V[64:128, s.par, TILES, :], V[64:128, s.par, 0, :]).then_inc(sig["v_mix"], 1)

                def square_sums(s, t):
                    dve.wait_ge(sig[f"qk_sq{t}"], s.n + 1)
                    dve.wait_ge(sig[f"qk_na{t}"], s.n)
                    dve.wait_ge(sig[f"qk_ln{t}"], s.n)
                    v.tensor_reduce(ss[:, t, :], heads(qk_sq[:], 2 * HEADS), AX.X, ALU.add).then_inc(sig[f"qk_ss{t}"], 1)

                def clip(s, t):
                    dve.wait_ge(sig[f"qk_ss{t}"], s.n + 1)
                    v.tensor_scalar(ss[:, t, :], ss[:, t, :], 1e-24, None, ALU.max).then_inc(sig[f"qk_clip{t}"], 1)

                def newton_a(s, t):
                    dve.wait_ge(sig[f"qk_r{t}"], s.n + 1)
                    dve.wait_ge(sig[f"qk_nc{t}"], s.n)
                    v.tensor_tensor(nwt[:, t, :], ss[:, t, :], rn[:, t, :], ALU.mult).then_inc(sig[f"qk_na{t}"], 1)

                def newton_b(s, t):
                    dve.wait_ge(sig[f"qk_na{t}"], s.n + 1)
                    v.scalar_tensor_tensor(nwt[:, t, :], nwt[:, t, :], -0.5, rn[:, t, :], ALU.mult, ALU.mult)\
                        .then_inc(sig[f"qk_nb{t}"], 1)

                def newton_c(s, t):
                    dve.wait_ge(sig[f"qk_nb{t}"], s.n + 1)
                    v.scalar_tensor_tensor(rn[:, t, :], nwt[:, t, :], 1.5, rn[:, t, :], ALU.add, ALU.mult)\
                        .then_inc(sig[f"qk_nc{t}"], 1)

                def normed(s, t):
                    dve.wait_ge(sig[f"qk_nc{t}"], s.n + 1)
                    dve.wait_ge(sig[f"rot_u{t}"], s.n)
                    dve.wait_ge(sig[f"rot_w{t}"], s.n)
                    v.tensor_tensor(heads(qk_n[:, t, :], 2 * HEADS), two(f"q_proj{t}").rearrange("p b (h d) -> p (b h) d", h=HEADS),
                                    rn[:, t, :].unsqueeze(2).broadcast_to([128, 2 * HEADS, DH]),
                                    ALU.mult).then_inc(sig[f"qk_n{t}"], 1)

                def k_transposed(s, t):
                    dve.wait_ge(sig[f"kT_mm{t}"], s.n + 1)
                    dve.wait_ge(sig["s_mm0"], s.n)
                    dve.wait_ge(sig["s_mm1"], s.n)
                    v.tensor_copy(kT[:, :, 128 * t:128 * t + 128], pairs(f"kT_mm{t}")).then_inc(sig[f"kT{t}"], 1)

                def maxes(s, t):
                    dve.wait_ge(sig[f"s_mm{t}"], s.n + 1)
                    dve.wait_ge(sig[f"s_exp{t}"], s.n)
                    v.tensor_reduce(nmax[:, t, :], two(f"s_mm{t}").rearrange("p b (c k) -> p (b c) k", c=4),
                                    AX.X, ALU.max, negate=True).then_inc(sig[f"s_max{t}"], 1)

                def sums(s, t):
                    dve.wait_ge(sig[f"s_exp{t}"], s.n + 1)
                    dve.wait_ge(sig[f"s_norm{t}"], s.n)
                    v.reciprocal(lrec[:, t, :], lsum[:, t, :]).then_inc(sig[f"s_rec{t}"], 1)

                def normalise(s, t):
                    dve.wait_ge(sig[f"s_rec{t}"], s.n + 1)
                    v.tensor_tensor(prob[:, t], prob[:, t], lrec[:, t, :].unsqueeze(2).broadcast_to([128, HEADS, 128]),
                                    ALU.mult).then_inc(sig[f"s_norm{t}"], 1)

                def prob_copy(s, t, half):
                    dve.wait_ge(sig[f"pT_mm{t}{half}"], s.n + 1)
                    dve.wait_ge(sig["oT_mm0"] if t else sig["oT_mm1"], s.n + t)
                    v.tensor_copy(pT[:, 4 * half:4 * half + 4, :], pairs(f"pT_mm{t}{half}")).then_inc(sig[f"pT{t}{half}"], 1)

                def attended_low(s, t):
                    dve.wait_ge(sig[f"oT{t}"], s.n + 1)
                    dve.wait_ge(sig["wo_mm"], s.n)
                    o = slice(128 * t, 128 * t + 128)
                    v.tensor_tensor(oT_lo[:, :, o], pairs(f"oT_mm{t}"), oT[:, :, o].bitcast(F32), ALU.subtract)\
                        .then_inc(sig[f"o_lo{t}"], 1)

                def residual_attn(s):
                    dve.wait_ge(sig["wo_mm"], s.n + 1)
                    x = X[:, bass.ds(s.col, L)]
                    v.tensor_tensor(x, half("wo_mm"), x, ALU.add).then_inc(sig["x_attn"], 1)

                def shift(s):
                    dve.wait_ge(sig["x_attn"], s.n + 1)
                    dve.wait_ge(sig["c_dev"], s.n)
                    for rows, src, dst in shifted(s.col):
                        last = v.tensor_scalar(hs[rows, dst], X[rows, src], 1.0, None, ALU.mult)
                    last.then_inc(sig["c_shift"], 1)

                def c_deviation(s):
                    dve.wait_ge(sig["c_mean"], s.n + 1)
                    dve.wait_ge(sig["c_lo"], s.n)
                    v.tensor_tensor(dev[:], hs[:], half("c_mean"), ALU.subtract).then_inc(sig["c_dev"], 1)

                def c_newton_a(s):
                    dve.wait_ge(sig["c_rstd"], s.n + 1)
                    dve.wait_ge(sig["c_aff"], s.n)
                    v.scalar_tensor_tensor(cnwt[:], half("c_var"), LN_EPS, crstd[:], ALU.add, ALU.mult).then_inc(sig["c_na"], 1)

                def c_newton_b(s):
                    dve.wait_ge(sig["c_na"], s.n + 1)
                    v.scalar_tensor_tensor(cnwt[:], cnwt[:], -0.5, crstd[:], ALU.mult, ALU.mult).then_inc(sig["c_nb"], 1)

                def c_newton_c(s):
                    dve.wait_ge(sig["c_nb"], s.n + 1)
                    v.scalar_tensor_tensor(cnwt[:], cnwt[:], 1.5, crstd[:], ALU.add, ALU.mult).then_inc(sig["c_nc"], 1)

                def c_normalised(s):
                    dve.wait_ge(sig["c_nc"], s.n + 1)
                    v.tensor_tensor(xn[:], cnwt[:], dev[:], ALU.mult).then_inc(sig["c_xn"], 1)

                def c_affine(s):
                    dve.wait_ge(sig["c_xn"], s.n + 1)
                    v.tensor_scalar(hn[:], xn[:], lvec[:, s.layer, 0:1], lvec[:, s.layer, 1:2],
                                    ALU.mult, ALU.add).then_inc(sig["c_aff"], 1)

                def c_low(s):
                    dve.wait_ge(sig["c_hi"], s.n + 1)
                    dve.wait_ge(sig["c_up1"], s.n)
                    v.tensor_tensor(f_lo[:], hn[:], f_hi[:].bitcast(F32), ALU.subtract).then_inc(sig["c_lo"], 1)

                def geglu(s, k):
                    m = CHUNKS[k][1]
                    dve.wait_ge(sig[f"c_gelu{k}"], s.n + 1)
                    dve.wait_ge(sig["c_down"], s.n)
                    v.scalar_tensor_tensor(act_[0:m, k, :], ps[0:m, BANK[f"c_up{k}"], L:2 * L], b1s[0:m, s.layer, 0, k:k + 1],
                                           gel[0:m, k, :], ALU.add, ALU.mult).then_inc(sig[f"c_act{k}"], 1)

                def residual_ffn(s):
                    dve.wait_ge(sig["c_down"], s.n + 1)
                    x = X[:, bass.ds(s.col, L)]
                    v.scalar_tensor_tensor(x, half("c_down"), lvec[:, s.layer, 2:3], x, ALU.add, ALU.add).then_inc(sig["x_ffn"], 1)

                def output(s):
                    if s.layer == DEPTH - 1:
                        dve.wait_ge(sig["x_ffn"], s.n + 1)
                        cols = bass.ds(s.col, L)
                        v.scalar_tensor_tensor(X1[:, cols], X[:, cols], mod[:, 5, bass.ds(s.item, 1)], X1[:, cols],
                                               ALU.mult, ALU.add).then_inc(sig["o_comp"], 1)

                if st[1].on: newton_c(st[1], 0)
                if st[1].on: normed(st[1], 0)
                if st[2].on: k_transposed(st[2], 1)
                if st[4].on: c_newton_b(st[4])
                if st[2].on: sums(st[2], 0)
                if st[4].on: c_newton_c(st[4])
                if st[4].on: c_normalised(st[4])
                if st[3].on: attended_low(st[3], 1)
                if st[1].on: square_sums(st[1], 1)
                if st[4].on: c_affine(st[4])
                if st[1].on: clip(st[1], 1)
                if st[0].on: h_high(st[0])
                if st[2].on: maxes(st[2], 1)
                if st[1].on: newton_a(st[1], 1)
                if st[2].on: prob_copy(st[2], 0, 0)
                if st[1].on: newton_b(st[1], 1)
                if st[4].on: c_low(st[4])
                if st[1].on: newton_c(st[1], 1)
                if st[3].on: residual_attn(st[3])
                if st[1].on: normed(st[1], 1)
                if st[3].on: shift(st[3])
                if st[5].on: residual_ffn(st[5])
                if st[0].on: h_low(st[0])
                if st[5].on: output(st[5])
                if st[2].on: sums(st[2], 1)
                if st[2].on: attended_low(st[2], 0)
                if st[3].on: c_deviation(st[3])
                if st[2].on: normalise(st[2], 1)
                if st[4].on: geglu(st[4], 2)
                if st[1].on: mixed(st[1])
                if st[4].on: geglu(st[4], 0)
                if st[0].on: square_sums(st[0], 0)
                if st[4].on: geglu(st[4], 1)
                if st[0].on: clip(st[0], 0)
                if st[1].on: maxes(st[1], 0)
                if st[0].on: newton_a(st[0], 0)
                if st[3].on: c_newton_a(st[3])
                if st[0].on: newton_b(st[0], 0)
            layers(dve, step)
        @block.gpsimd
        def _(pool):
            g = nc.gpsimd
            raise_once(pool, STEPPED["gpsimd"])
            pool.wait_ge(sig["tables_in"], 16 * N_TABLES)
            pool.wait_ge(sig["w_in"], 16 * W_LOADS * DEPTH)
            for l in range(DEPTH):
                g.tensor_scalar(wq_hi[l][:], wq_raw[l], 1.0, None, ALU.mult)
                g.tensor_scalar(flat(wo_hi[l][:]), wo_raw[l], 1.0, None, ALU.mult)
                g.tensor_scalar(w1_hi[l][:], w1_raw[l], 1.0, None, ALU.mult).then_inc(sig["w_hi"], 1)
                for t in range(TILES):
                    g.tensor_tensor(rot[:, l, t, 0:2, :], tab[:, t, 0:2, :], qks[:, l], ALU.mult)
                    for j in range(2):
                        g.tensor_tensor(heads(rot[:, l, t, 2 + j, :], 2), heads(tab[:, t, 2 + j, :], 2),
                                        heads(qks[:, l, j, :], 2)[:, ::-1, :], ALU.mult)
                pool.wait_ge(sig["w_hi"], l + 1)
                g.tensor_tensor(wq_lo[l][:], wq_raw[l], wq_hi[l][:].bitcast(F32), ALU.subtract)
                g.tensor_tensor(flat(wo_lo[l][:]), wo_raw[l], flat(wo_hi[l][:]).bitcast(F32), ALU.subtract)
                g.tensor_tensor(w1_lo[l][:], w1_raw[l], w1_hi[l][:].bitcast(F32), ALU.subtract)\
                    .then_inc(sig["w_ready"], 1)

            pool.wait_ge(sig["w_ready"], DEPTH)

            def step(*st):
                def rotate_cos(s, t):
                    table = rot[:, s.layer, t]
                    pool.wait_ge(sig[f"qk_n{t}"], s.n + 1)
                    pool.wait_ge(sig[f"qT_mm{t}"], s.n)
                    pool.wait_ge(sig[f"kT_mm{t}"], s.n)
                    for j in range(2):
                        o = slice(INNER * j, INNER * j + INNER)
                        last = g.tensor_tensor(heads(qk_u[:, t, o], HEADS), heads(qk_n[:, t, o], HEADS),
                                               table[:, j, :].unsqueeze(1).broadcast_to([128, HEADS, DH]), ALU.mult)
                    last.then_inc(sig[f"rot_u{t}"], 1)

                def rotate_sin(s, t):
                    table = rot[:, s.layer, t]
                    pool.wait_ge(sig[f"qk_n{t}"], s.n + 1)
                    pool.wait_ge(sig["rot0"] if t else sig["rot1"], s.n + t)
                    for j in range(2):
                        o = slice(INNER * j, INNER * j + INNER)
                        for half in range(2):
                            a, b = slice(32 * half, 32 * half + 32), slice(32 - 32 * half, 64 - 32 * half)
                            last = g.tensor_tensor(heads(qk_w[:, o], HEADS)[:, :, a], heads(qk_n[:, t, o], HEADS)[:, :, b],
                                                   table[:, 2 + j, a].unsqueeze(1).broadcast_to([128, HEADS, 32]), ALU.mult)
                    last.then_inc(sig[f"rot_w{t}"], 1)

                def rotate_add(s, t):
                    pool.wait_ge(sig[f"rot_u{t}"], s.n + 1)
                    pool.wait_ge(sig[f"rot_w{t}"], s.n + 1)
                    g.tensor_tensor(qk_u[:, t, :], qk_u[:, t, :], qk_w[:], ALU.add).then_inc(sig[f"rot{t}"], 1)

                def normalise(s, t):
                    pool.wait_ge(sig[f"s_rec{t}"], s.n + 1)
                    g.tensor_tensor(prob[:, t], prob[:, t], lrec[:, t, :].unsqueeze(2).broadcast_to([128, HEADS, 128]),
                                    ALU.mult).then_inc(sig[f"s_norm{t}"], 1)

                if st[3].on: rotate_cos(st[3], 0)
                if st[4].on: normalise(st[4], 0)
                if st[3].on: rotate_sin(st[3], 0)
                if st[3].on: rotate_add(st[3], 0)
                if st[3].on: rotate_cos(st[3], 1)
                if st[3].on: rotate_sin(st[3], 1)
                if st[3].on: rotate_add(st[3], 1)
            layers(pool, step)


def kernel(**inputs):
    import numpy as np
    import ml_dtypes
    import concourse.bacc as bacc
    from concourse.bass_utils import run_bass_kernel_spmd

    def t(name):
        return np.asarray(inputs[name])

    half = np.arange(0, DH, 2, dtype=np.float32)
    freqs = np.arange(L, dtype=np.float32)[:, None] * (1.0 / 10000.0 ** (half / DH)).astype(np.float32)[None, :]
    base = (half + 0.4 * DH) / (1.4 * DH)
    scale = base[None, :] ** ((np.arange(L) - L // 2) / float(WIN // 2))[:, None]
    cos, sin, scale = (np.concatenate([a, a], -1) for a in (np.cos(freqs), np.sin(freqs), scale))
    sin = sin * np.where(np.arange(DH) < DH // 2, -1.0, 1.0)[None, :]
    rot_tab = np.stack([8.0 * cos * scale, cos / scale, 8.0 * sin * scale, sin / scale], 1).astype(np.float32)
    rot_tab = rot_tab.reshape(TILES, 128, 4, DH).transpose(1, 0, 2, 3)
    row, slot = np.arange(128)[:, None], np.arange(128)[None, :]
    keys = np.stack([np.broadcast_to(slot, (128, 128)),
                     np.where((row < 64) & (slot >= 64), slot, slot + 128)])
    query = np.stack([np.broadcast_to(row, (128, 128)), np.broadcast_to(row + 128, (128, 128))])
    seen = (keys <= query) & (query <= keys + WIN)
    mask = np.where(seen, 0.0, -1e30).transpose(1, 0, 2)
    mask = np.tile(mask, (1, 1, 4)).astype(ml_dtypes.bfloat16)

    arrays = {
        "xT": t("L0_attn_x").reshape(TOK, D).T, "cT": t("L0_c").T, "wmod": t("L0_wmod"),
        "w_inT": t("L0_attn_W_in").T, "w_x0": t("L0_attn_W_x")[0:1], "w_dt": t("L0_attn_W_dt").reshape(1, D),
        "b_dt": t("L0_attn_b_dt").reshape(D, 1), "gamma": t("L0_attn_gamma").reshape(D, 1),
        "beta": t("L0_attn_beta").reshape(D, 1),
        "wqkv": t("L0_ffn_wqkv"), "q_scale": t("L0_ffn_q_scale"), "k_scale": t("L0_ffn_k_scale"),
        "wo": t("L0_ffn_wo"), "ln_g": t("L0_ffn_ln_g"), "ln_b": t("L0_ffn_ln_b"), "w1": t("L0_ffn_w1"),
        "b1": t("L0_ffn_b1"), "w2": t("L0_ffn_w2"), "b2": t("L0_ffn_b2"),
        "rot_tab": rot_tab, "mask": mask, "ident_bf": np.eye(128, dtype=ml_dtypes.bfloat16),
        "ident": np.eye(128, dtype=np.float32),
    }
    nc = bacc.Bacc("TRN2", target_bir_lowering=False, num_devices=1)
    feeds, args = {}, {}
    for name, a in arrays.items():
        a = np.ascontiguousarray(a)
        feeds[f"in_{name}"] = a
        args[name] = nc.dram_tensor(f"in_{name}", a.shape, mybir.dt.from_np(a.dtype), kind="ExternalInput").ap()
    args["outT"] = nc.dram_tensor("outT", (D, TOK), F32, kind="ExternalOutput").ap()
    build(nc, **args)
    r = run_bass_kernel_spmd(nc, [feeds], core_ids=[0])
    return np.ascontiguousarray(r.results[0]["outT"].T).reshape(SEQS, L, D)
```
